# Optimizing a Trainium2 kernel written in Bass

```python
import numpy as np
import jax
import jax.numpy as jnp

def _softmax(x, axis=-1):
    return jax.nn.softmax(x, axis=axis)

def _gelu(x):
    return jax.nn.gelu(x, approximate=True)

def _silu(x):
    return jax.nn.silu(x)

def _sigmoid(x):
    return jax.nn.sigmoid(x)

def _layernorm(x, axis=-1, eps=1e-05):
    m = jnp.mean(x, axis=axis, keepdims=True)
    v = jnp.var(x, axis=axis, keepdims=True)
    return (x - m) / jnp.sqrt(v + eps)

def _scatter_add(tgt, idx, src, axis=0):
    return tgt.at[idx].add(src)

def _segment_sum(src, seg, n):
    return jax.ops.segment_sum(src, seg, n)
kernel_name = 'mk_flamingo_gated_d1_seqx_r8_1ed11f'

def setup_inputs(seed: int=0):
    np.random.seed(seed)
    _w = jnp.asarray

    def _rec_inputs():
        import jax
        import jax.numpy as jnp
        _rk = jax.random.key(seed)
        x = 7.22e-05 + 1 * jax.random.normal(jax.random.fold_in(_rk, 1), (32, 128, 128), jnp.float32)
        _lenS = 128 - jax.random.randint(jax.random.fold_in(_rk, 7), (32,), 0, max(1, 128 // 4) + 1, jnp.int32)
        _lenS2 = 128 - jax.random.randint(jax.random.fold_in(_rk, 8), (32,), 0, max(1, 128 // 4) + 1, jnp.int32)
        _ctx_1024P = jax.random.normal(jax.random.fold_in(_rk, 11), (32, 16, 128), jnp.float32)
        _ctx_1024c = jax.random.dirichlet(jax.random.fold_in(_rk, 511), 0.3 * jnp.ones((16,), jnp.float32), (32, 128))
        _ctx_1024t = jnp.einsum('bsk,bkd->bsd', _ctx_1024c, _ctx_1024P)
        _ctx_1024t = _ctx_1024t * jax.lax.rsqrt(jnp.mean(jnp.square(_ctx_1024t)) + 1e-12) * 0.953939
        ctx_1024 = 4.13588e-05 + 0.999923 * (_ctx_1024t + 0.3 * jax.random.normal(jax.random.fold_in(_rk, 611), (32, 128, 128), jnp.float32))
        _g = jax.random.normal(jax.random.fold_in(_rk, 9001), (2, 1), jnp.float32)
        _g = jnp.sign(_g) * jnp.maximum(jnp.abs(_g), 1.0) + (_g == 0) * 1.0
        g_xattn = _g[0]
        g_ffn = _g[1]
        return (x, ctx_1024, g_xattn, g_ffn)
    x, ctx_1024, g_xattn, g_ffn = _rec_inputs()

    def _L0_xattn_setup():
        import jax, jax.numpy as jnp
        import numpy as np
        import math
        B, Q, K = (4, 256, 256)
        D_QUERY = D_KEY = 128
        N_HEAD, D_HIDDEN, D_OUT = (16, 64, 128)

        def _xavier(key, shape):
            fan_out, fan_in = shape
            a = math.sqrt(6.0 / (fan_in + fan_out))
            return jax.random.uniform(key, shape, jnp.float32, -a, a)
        key = jax.random.key(seed)
        ks = jax.random.split(key, 6)
        query = jax.random.normal(ks[0], (B, Q, D_QUERY), jnp.float32)
        key_t = jax.random.normal(ks[1], (B, K, D_KEY), jnp.float32)
        value = jax.random.normal(ks[2], (B, K, D_KEY), jnp.float32)
        Wq = _xavier(ks[3], (N_HEAD * D_HIDDEN, D_QUERY))
        Wk = _xavier(ks[4], (N_HEAD * D_HIDDEN, D_KEY))
        Wv = _xavier(ks[5], (N_HEAD * D_HIDDEN, D_KEY))
        ko = jax.random.split(ks[5], 2)
        Wo = 0.02 * jax.random.normal(ko[0], (D_OUT, N_HEAD * D_HIDDEN), jnp.float32)
        bo = 0.02 * jax.random.normal(ko[1], (D_OUT,), jnp.float32)
        return {'query': query, 'key': key_t, 'value': value, 'Wq': Wq, 'Wk': Wk, 'Wv': Wv, 'Wo': Wo, 'bo': bo}
    _L0_xattn_all = _L0_xattn_setup()
    _L0_xattn_in = {k: v for k, v in _L0_xattn_all.items() if k in ('Wq', 'Wk', 'Wv', 'Wo', 'bo')}
    del _L0_xattn_all

    def _L0_ffn_setup():
        import jax, jax.numpy as jnp
        import numpy as np
        TOP_K = 2
        key = jax.random.key(seed)
        k0, k1, k2, k3, k4 = jax.random.split(key, 5)
        B, S, D, H, E = (4, 256, 128, 256, 8)
        x = jax.random.normal(k0, (B, S, D), dtype=jnp.float32)
        router_w = jax.random.normal(k1, (E, D), dtype=jnp.float32) * D ** (-0.5)
        w_gate = jax.random.normal(k2, (E, D, H), dtype=jnp.float32) * D ** (-0.5)
        w_up = jax.random.normal(k3, (E, D, H), dtype=jnp.float32) * D ** (-0.5)
        w_down = jax.random.normal(k4, (E, H, D), dtype=jnp.float32) * H ** (-0.5)
        return {'x': x, 'router_w': router_w, 'w_gate': w_gate, 'w_up': w_up, 'w_down': w_down}
    _L0_ffn_all = _L0_ffn_setup()
    _L0_ffn_in = {k: v for k, v in _L0_ffn_all.items() if k in ('router_w', 'w_gate', 'w_up', 'w_down')}
    del _L0_ffn_all
    return {'x': x, 'ctx_1024': ctx_1024, 'g_xattn': g_xattn, 'g_ffn': g_ffn, 'L0_xattn_Wq': _L0_xattn_in['Wq'], 'L0_xattn_Wk': _L0_xattn_in['Wk'], 'L0_xattn_Wv': _L0_xattn_in['Wv'], 'L0_xattn_Wo': _L0_xattn_in['Wo'], 'L0_xattn_bo': _L0_xattn_in['bo'], 'L0_ffn_router_w': _L0_ffn_in['router_w'], 'L0_ffn_w_gate': _L0_ffn_in['w_gate'], 'L0_ffn_w_up': _L0_ffn_in['w_up'], 'L0_ffn_w_down': _L0_ffn_in['w_down']}

def reference(x, ctx_1024, g_xattn, g_ffn, L0_xattn_Wq, L0_xattn_Wk, L0_xattn_Wv, L0_xattn_Wo, L0_xattn_bo, L0_ffn_router_w, L0_ffn_w_gate, L0_ffn_w_up, L0_ffn_w_down):
    import jax
    import jax.numpy as jnp

    def _L0_xattn_ref(query, key, value, Wq, Wk, Wv, Wo, bo):
        import jax, jax.numpy as jnp
        import numpy as np
        import math
        B, Q, K = (4, 256, 256)
        D_QUERY = D_KEY = 128
        N_HEAD, D_HIDDEN, D_OUT = (16, 64, 128)

        def _xavier(key, shape):
            fan_out, fan_in = shape
            a = math.sqrt(6.0 / (fan_in + fan_out))
            return jax.random.uniform(key, shape, jnp.float32, -a, a)
        scaling = 1.0 / math.sqrt(D_HIDDEN)
        b, q = query.shape[:2]
        k = key.shape[1]
        qh = (query @ Wq.T).reshape(b, q, N_HEAD, D_HIDDEN) * scaling
        kh = (key @ Wk.T).reshape(b, k, N_HEAD, D_HIDDEN)
        vh = (value @ Wv.T).reshape(b, k, N_HEAD, D_HIDDEN)
        attn = jnp.einsum('bqhd,bkhd->bhqk', qh, kh)
        attn = jax.nn.softmax(attn, axis=-1)
        out = jnp.einsum('bhqk,bkhd->bqhd', attn, vh).reshape(b, q, N_HEAD * D_HIDDEN)
        return out @ Wo.T + bo

    def _L0_ffn_ref(x, router_w, w_gate, w_up, w_down):
        import jax, jax.numpy as jnp
        import numpy as np
        TOP_K = 2
        B, S, D = x.shape
        E = router_w.shape[0]
        xt = x.reshape(-1, D)
        logits = xt @ router_w.T
        topk_vals, topk_idx = jax.lax.top_k(logits, TOP_K)
        g = jax.nn.sigmoid(topk_vals)
        g = g / (g.sum(axis=-1, keepdims=True) + 1e-10)
        out = jnp.zeros_like(xt)
        for e in range(E):
            ge = jnp.sum(jnp.where(topk_idx == e, g, jnp.zeros_like(g)), axis=-1)
            h = jax.nn.silu(xt @ w_gate[e]) * (xt @ w_up[e])
            out = out + ge[:, None] * (h @ w_down[e])
        return out.reshape(B, S, D)
    x = x + jnp.tanh(g_xattn[0]) * _L0_xattn_ref(_layernorm(x, axis=-1), ctx_1024, ctx_1024, L0_xattn_Wq, L0_xattn_Wk, L0_xattn_Wv, L0_xattn_Wo, L0_xattn_bo)
    x = x + jnp.tanh(g_ffn[0]) * _L0_ffn_ref(_layernorm(x, axis=-1), L0_ffn_router_w, L0_ffn_w_gate, L0_ffn_w_up, L0_ffn_w_down)
    return x

_drawn_inputs = setup_inputs


def setup_inputs(seed=0):
    import zlib

    import numpy as np

    out = dict(_drawn_inputs(seed))
    spreads = {}
    factors = {}
    for name, (base, spread) in spreads.items():
        noise = np.random.default_rng([zlib.crc32(name.encode()), seed]).standard_normal(out[name].shape)
        drawn = base * np.exp(spread * noise) if base else spread * noise
        out[name] = jnp.asarray(drawn.astype(out[name].dtype))
    for name, factor in factors.items():
        out[name] = (out[name] * factor).astype(out[name].dtype)
    return out
```

```python
from contextlib import ExitStack

import concourse.bass as bass
from concourse import mybir

F32 = mybir.dt.float32
F32R = mybir.dt.float32r
ALU = mybir.AluOpType
ACT = mybir.ActivationFunctionType
AX = mybir.AxisListType

P = 128
B = 32
H, HD = 16, 64
NCH = H * HD // P
E, F = 8, 256
FC = F // P
EPS = 1e-5
ROOT_STEPS = 5
SCALE = 1.0 / HD ** 0.5
VW = HD + 1

UB = 2
BU = 2
BB = UB * BU
OB = 2
STEPS = BB * OB
NBODY = B // BB
NOCT = B * OB
NUNIT = B // UB

GT = 4
NG = B // GT
TOP_STEPS = 11


def fills_at(j, first, last):
    q, bb, even = j % (UB * OB), j // OB, j % OB == 0
    slots = {"A": [], "B": [], "C": []}
    if even and not (first and bb < 2):
        slots["A"].append(("X2T", 0, bb - 2))
    if not even and not (first and bb < 1):
        slots["A"].append(("OP", 0, bb - 1))
    if not (last and j >= UB * OB):
        ahead = {
            0: {"A": [("XT", 0)], "C": [("QK", 0)]},
            1: {"A": [("QK", 1)], "B": [("QK", 2)], "C": [("QK", 3), ("QK", 4)]},
            2: {"A": [("QK", 5)], "B": [("QK", 6)], "C": [("QK", 7), ("V", 0)]},
            3: {"A": [("V", 1)], "B": [("V", 2)], "C": [("V", 3)]},
        }[q]
        for s, parts in ahead.items():
            slots[s] += [(name, part, None) for name, part in parts]
    if even and not (first and bb < 1):
        slots["B"].append(("OT", 0, bb - 1))
        slots["C"].append(("OT", 1, bb - 1))
    if even and not (first and bb < 2):
        slots["C"].append(("LG", 0, bb - 2))
    return slots


def fills_of(first, last):
    return [(j, s, n) for j in range(STEPS) for s, parts in fills_at(j, first, last).items() for n, _ in enumerate(parts)]


SETUP = 4 * 2 + 1
AHEAD = 1 + 8 + 4
N_FIRST = len(fills_of(True, False))
N_MID = len(fills_of(False, False))
N_LAST = len(fills_of(False, True))
assert N_MID % 2 == 0
BASE = SETUP + AHEAD + N_FIRST - N_MID
TAIL = BASE + N_MID * (NBODY - 1) + N_LAST


class Fill:

    def __init__(self, fixed, it=0):
        self.bank = fixed % 2
        self.full = N_MID * it + (fixed + 1)
        self.moved = (N_MID // 2) * it + (fixed // 2 + 1)
        self.before = None if isinstance(it, int) and it == 0 and fixed < 2 else (N_MID // 2) * it + fixed // 2
        self.order = fixed


class Body:

    def __init__(self, it, first=False, last=False):
        self.it, self.first, self.last = it, first, last
        self.plan = fills_of(first, last)

    def slot(self, j, s):
        return [(name, part, bb, self.fill(self.plan.index((j, s, n))))
                for n, (name, part, bb) in enumerate(fills_at(j, self.first, self.last)[s])]

    def fill(self, at):
        return Fill(SETUP + AHEAD + at) if self.first else Fill(BASE + at, self.it)

    def find(self, name, part, steps):
        for j in steps:
            kind = (False, False) if j < 0 else (self.first, self.last)
            for s, parts in fills_at(j % STEPS, *kind).items():
                for n, entry in enumerate(parts):
                    if entry[:2] == (name, part):
                        at = fills_of(*kind).index((j % STEPS, s, n))
                        return Fill(BASE - N_MID + at, self.it) if j < 0 else self.fill(at)

    def ahead(self, name, part, us):
        if us == 0 and self.first:
            return prologue_fill(name, part)
        return self.find(name, part, range(4 * (us - 1), 4 * us))

    def octet(self, j):
        return STEPS * self.it + j

    def batch(self, bb):
        return BB * self.it + bb

    def unit(self, us):
        return BU * self.it + us


def prologue_fill(name, part):
    return Fill(SETUP + {"XT": 0, "QK": 1, "V": 9}[name] + part)


def build(nc, x, ctxt, g_xattn, g_ffn, Wq, Wk, Wv, Wo, bo, router_w, w_gate, w_up, w_down, out):
    with ExitStack() as ctx:
        def sb(name, shape, dt=F32):
            return ctx.enter_context(nc.sbuf_tensor(name, shape, dt))

        def ps(name):
            return ctx.enter_context(nc.psum_tensor(name, [P, 512], F32))

        def sem(name):
            return ctx.enter_context(nc.semaphore(name))

        ident = sb("ident", [P, P])
        gates = sb("gates", [P, 2])
        tgates = sb("tgates", [P, 2])
        bo_b = sb("bo_b", [P, P])
        bo_t = sb("bo_t", [P, P])
        rw_in = sb("rw_in", [E, P])
        rwT = sb("rwT", [P, E])
        w_hi = [sb(f"w{c}_hi", [P, NCH * P], F32R) for c in "qkv"]
        w_lo = [sb(f"w{c}_lo", [P, NCH * P], F32R) for c in "qkv"]
        woT = sb("woT", [P, NCH, P])
        wgu_hi = sb("wgu_hi", [P, E, 2 * F], F32R)
        wgu_lo = sb("wgu_lo", [P, E, 2 * F], F32R)
        wd = sb("wd", [P, E, FC, P])
        x1_all = sb("x1_all", [P, B * P])
        gu_stage = x1_all[:, B * P - 4 * F:B * P].rearrange("p (s f) -> p s f", s=2)
        x2T_hi = sb("x2T_hi", [P, B * P], F32R)
        x2T_lo = sb("x2T_lo", [P, B * P], F32R)
        lg_all = sb("lg_all", [P, B * E])
        x_in = [sb(f"x_in{i}", [P, UB, P]) for i in range(2)]
        c_in = [sb(f"c_in{i}", [P, UB, P]) for i in range(2)]
        xn = [sb(f"xn{i}", [P, UB, P]) for i in range(2)]
        st1 = sb("st1", [P, UB, 6])
        mv1 = sb("mv1", [P, UB, 2])
        ve1, rs1, nt1 = (sb(s, [P, UB]) for s in ("ve1", "rs1", "nt1"))
        xcT_hi = sb("xcT_hi", [P, 2 * UB * P], F32R)
        xcT_lo = sb("xcT_lo", [P, 2 * UB * P], F32R)
        qk = [[sb(f"{c}T{i}", [P, NCH, UB * P]) for c in "qk"] for i in range(2)]
        v = sb("v", [P, BB, H, VW])
        mx = [sb(f"mx{c}", [P, 4]) for c in "ab"]
        p_buf = sb("p_buf", [P, 2, 2, 512])
        pT_buf = sb("pT_buf", [P, 2, 2, 512])
        w_stage = [(p_buf, pT_buf)[w // 2][:, w % 2, :, :].rearrange("p a b -> p (a b)")
                   .rearrange("p (c d) -> p c d", c=NCH) for w in range(4)]
        rden = [sb(f"rden{c}", [P, 4]) for c in "ab"]
        o_n = sb("o_n", [P, H, HD])
        oT = sb("oT", [P, NCH * P])
        st2 = sb("st2", [P, 6])
        mv2 = sb("mv2", [P, 2])
        minus_half = sb("minus_half", [P, UB])
        ve2, rs2, nt2 = (sb(s, [P, 1]) for s in ("ve2", "rs2", "nt2"))
        x2 = sb("x2", [P, P])
        x2T = sb("x2T", [P, P])
        first_wins = sb("first_wins", [P, B, E])
        top = sb("top", [P, 2, B])
        free_q = qk[0][0][:, :, :].rearrange("p c t -> p (c t)")

        def per_expert(i):
            return free_q[:, i * B * E:(i + 1) * B * E].rearrange("p (b e) -> p b e", e=E)

        one = [per_expert(0), per_expert(1)]
        r_tmp = per_expert(2)
        r_max = sb("r_max", [P, B])
        gate_e = sb("gate_e", [P, 2, B])
        gate_s = sb("gate_s", [P, 2, B])
        gate_n = sb("gate_n", [P, B])
        ge_all = per_expert(3)
        ge_now = sb("ge_now", [P, GT * E])
        v_flat = v[:, :, :, :].rearrange("p b h w -> p (b h w)")
        hid = [[v_flat[:, (2 * i + c) * 512:(2 * i + c + 1) * 512] for c in range(FC)] for i in range(2)]
        silu = [v_flat[:, (4 + i) * 512:(5 + i) * 512] for i in range(2)]
        acc = v_flat[:, 6 * 512:7 * 512]
        out_sb = free_q[:, 4 * B * E:4 * B * E + GT * P]

        s_ps = [ps("sa"), ps("sb")]
        t_ps = [ps("ta"), ps("tb")]
        o_ps = [ps("oa"), ps("ob")]
        pj = [ps("pj0"), ps("pj1")]
        gate_ps, up_ps, y_ps = s_ps, t_ps, o_ps

        w_loaded = [sem(f"w{c}_loaded") for c in "qkvo"]
        small_loaded = sem("small_loaded")
        gates_ready = sem("gates_ready")
        bias_ready = sem("bias_ready")
        ident_ready = sem("ident_ready")
        consts_ready = sem("consts_ready")
        gu_loaded = [sem(f"gu_loaded{i}") for i in range(2)]
        gu_split = sem("gu_split")
        gu_hi_done = sem("gu_hi_done")
        wd_loaded = sem("wd_loaded")
        x_loaded = [sem(f"x_loaded{i}") for i in range(2)]
        c_loaded = [sem(f"c_loaded{i}") for i in range(2)]
        stats1, agg1, rstd1, xn_ready = (sem(s) for s in ("stats1", "agg1", "rstd1", "xn_ready"))
        root1, root2 = sem("root1"), sem("root2")
        xb_ready = sem("xb_ready")
        ctxT_taken = sem("ctxT_taken")
        pj_full = sem("pj_full")
        pj_moved = [sem(f"pj_moved{i}") for i in range(2)]
        w_hi_ready = sem("w_hi_ready")
        xcT_hi_ready = sem("xcT_hi_ready")
        scored = [sem(f"scored{c}") for c in "ab"]
        max_ready = [sem(f"max_ready{c}") for c in "ab"]
        shifted = [sem(f"shifted{c}") for c in "ab"]
        probs_ready = [sem(f"probs_ready{c}") for c in "ab"]
        transposed = [sem(f"transposed{c}") for c in "ab"]
        probsT_ready = [sem(f"probsT_ready{c}") for c in "ab"]
        pv_done = [sem(f"pv_done{c}") for c in "ab"]
        rden_ready = [sem(f"rden_ready{c}") for c in "ab"]
        o_ready = [sem(f"o_ready{c}") for c in "ab"]
        x1_ready, stats2, agg2, rstd2, x2_ready = (sem(s) for s in ("x1_ready", "stats2", "agg2", "rstd2", "x2_ready"))
        x2T_hi_done = sem("x2T_hi_done")
        x2T_split = sem("x2T_split")
        route = sem("route")
        gate_exp = sem("gate_exp")
        ge_ready = sem("ge_ready")
        gu_done = sem("gu_done")
        silu_done = sem("silu_done")
        hid_ready = sem("hid_ready")
        down_done = sem("down_done")
        acc_done = sem("acc_done")
        out_stored = sem("out_stored")
        passed = sem("passed")

        block = ctx.enter_context(nc.Block())

        def wait_moved(eng, fills):
            for bank in range(2):
                of = [f for f in fills if f.bank == bank]
                if of:
                    eng.wait_ge(pj_moved[bank], max(of, key=lambda f: f.order).moved)

        def wait_apart(eng, waited, value):
            eng.wait_ge(waited, value)
            eng.sem_inc(passed, 1)

        FIRST, LAST = Body(0, first=True), Body(NBODY - 1, last=True)

        @block.sync
        def _(sp):
            def load(u, par):
                sp.dma_start(x_in[par][:, :, :], x[bass.ds(u * UB, UB)].rearrange("b t d -> t b d"))\
                  .then_inc(x_loaded[par], 16)
                sp.dma_start(c_in[par][:, :, :], ctxt[bass.ds(u * UB, UB)].rearrange("b t d -> t b d"))\
                  .then_inc(c_loaded[par], 16)

            load(0, 0)
            sp.dma_start(w_stage[0], Wq.rearrange("(c p) d -> p c d", p=P)).then_inc(w_loaded[0], 16)
            sp.dma_start(w_stage[1], Wk.rearrange("(c p) d -> p c d", p=P)).then_inc(w_loaded[1], 16)
            sp.dma_start(w_stage[2], Wv.rearrange("(c p) d -> p c d", p=P)).then_inc(w_loaded[2], 16)
            load(1, 1)
            sp.dma_start(w_stage[3], Wo.rearrange("p (c d) -> p c d", d=P)).then_inc(w_loaded[3], 16)
            sp.dma_start(wd[:, :, :, :], w_down.rearrange("e (c p) d -> p e c d", p=P)).then_inc(wd_loaded, 16)
            with sp.Fori(1, NUNIT // 2) as i:
                for par in range(2):
                    sp.wait_ge(xn_ready, 2 * i + (par - 1))
                    sp.wait_ge(xb_ready, 2 * i + (par - 1))
                    sp.wait_ge(ctxT_taken, 2 * i + (par - 1))
                    load(2 * i + par, par)
            with sp.Fori(0, NG) as g:
                sp.wait_ge(acc_done, E * g + E)
                sp.dma_start(out[bass.ds(g * GT, GT)].rearrange("b t d -> t b d"),
                             out_sb.rearrange("p (b d) -> p b d", b=GT)).then_inc(out_stored, 16)
            sp.wait_ge(out_stored, 16 * NG)

        @block.gpsimd
        def _(pool):
            nc.gpsimd.memset(ident[:, :], 0.0).then_inc(consts_ready, 1)
            pool.wait_ge(consts_ready, 1)
            nc.gpsimd.affine_select(out=ident[:, :], in_=ident[:, :], compare_op=ALU.not_equal, fill=1.0,
                                    base=0, pattern=[[-1, P]], channel_multiplier=1).then_inc(ident_ready, 1)
            nc.gpsimd.memset(minus_half[:, :], -0.5).then_inc(consts_ready, 1)
            nc.gpsimd.memset(v[:, :, :, HD:VW], 1.0).then_inc(consts_ready, 1)
            for e in range(E):
                nc.gpsimd.memset(first_wins[:, :, e:e + 1], float(E - e)).then_inc(consts_ready, 1)

            def residual(u, par, arrived):
                pool.wait_ge(x_loaded[par], arrived)
                nc.gpsimd.tensor_tensor(x1_all[:, bass.ds(u * (UB * P), UB * P)].rearrange("p (b d) -> p b d", b=UB),
                                        x_in[par][:, :, :], bo_t[:, :].unsqueeze(1).to_broadcast([P, UB, P]),
                                        ALU.add).then_inc(xb_ready, 1)

            def split_x2(b, f):
                at = bass.ds(b * P, P)
                wait_moved(pool, [f])
                nc.gpsimd.tensor_copy(x2T_hi[:, at], x2T[:, :]).then_inc(x2T_hi_done, 1)
                pool.wait_ge(x2T_hi_done, b + 1)
                nc.gpsimd.tensor_tensor(x2T_lo[:, at], x2T[:, :], x2T_hi[:, at].bitcast(F32), ALU.subtract)\
                  .then_inc(x2T_split, 1)

            def inverse_root(k, n, counted, agg, chain, done, var, ve, rs, nt):
                at = [0]

                def step(op, last=False):
                    if last:
                        return op.then_inc(done, 1)
                    op.then_inc(chain, 1)
                    at[0] += 1
                    wait_apart(pool, chain, ROOT_STEPS * k + at[0])

                wait_apart(pool, agg, counted)
                step(nc.gpsimd.tensor_scalar(ve, var, EPS, None, ALU.add))
                step(nc.gpsimd.tensor_tensor(rs, ve, minus_half[:, 0:n], ALU.pow))
                step(nc.gpsimd.tensor_tensor(nt, ve, rs, ALU.mult))
                step(nc.gpsimd.tensor_tensor(nt, nt, rs, ALU.mult))
                step(nc.gpsimd.tensor_scalar(nt, nt, -0.5, 1.5, ALU.mult, ALU.add))
                step(nc.gpsimd.tensor_tensor(rs, rs, nt, ALU.mult), last=True)

            def root_x(u):
                inverse_root(u, UB, UB * (u + 1), agg1, root1, rstd1, mv1[:, :, 1], ve1[:, :], rs1[:, :], nt1[:, :])

            def root_x2(b):
                inverse_root(b, 1, b + 1, agg2, root2, rstd2, mv2[:, 1:2], ve2[:, :], rs2[:, :], nt2[:, :])

            pool.wait_ge(consts_ready, 3 + E)
            root_x(0)
            root_x(1)
            pool.wait_ge(bias_ready, 1)
            residual(0, 0, 16)
            residual(1, 1, 16)
            for e in range(E):
                pool.wait_ge(gu_loaded[e % 2], 32 * (e // 2 + 1))
                nc.gpsimd.tensor_copy(wgu_hi[:, e, :], gu_stage[:, e % 2, :]).then_inc(gu_hi_done, 1)
                pool.wait_ge(gu_hi_done, e + 1)
                nc.gpsimd.tensor_tensor(wgu_lo[:, e, :], gu_stage[:, e % 2, :], wgu_hi[:, e, :].bitcast(F32),
                                        ALU.subtract).then_inc(gu_split, 1)

            def body(bd):
                for j in range(STEPS):
                    if j % 4 == 2 and not bd.last:
                        us = j // 4
                        residual(bd.unit(us + 2), us, 16 * bd.it + 32)
                        root_x(bd.unit(us + 2))
                    for name, part, bb, f in bd.slot(j, "A"):
                        if name == "X2T":
                            split_x2(bd.batch(bb), f)
                        if name == "OP":
                            root_x2(bd.batch(bb))

            body(FIRST)
            with pool.Fori(1, NBODY - 1) as it:
                body(Body(it))
            body(LAST)
            split_x2(B - 2, Fill(TAIL))
            root_x2(B - 1)
            split_x2(B - 1, Fill(TAIL + 5))

        @block.scalar
        def _(act):
            act.dma_start(gates[:, 0:1], g_xattn.partition_broadcast(P)).then_inc(small_loaded, 16)
            act.dma_start(gates[:, 1:2], g_ffn.partition_broadcast(P)).then_inc(small_loaded, 16)
            act.dma_start(bo_b[:, :], bo.partition_broadcast(P)).then_inc(small_loaded, 16)
            act.dma_start(rw_in[:, :], router_w).then_inc(small_loaded, 16)
            act.wait_ge(small_loaded, 64)
            nc.scalar.activation(tgates[:, :], gates[:, :], ACT.Tanh).then_inc(gates_ready, 1)

            def load_gu(e):
                if e >= 2:
                    act.wait_ge(gu_split, e - 1)
                act.dma_start(gu_stage[:, e % 2, 0:F], w_gate[e]).then_inc(gu_loaded[e % 2], 16)
                act.dma_start(gu_stage[:, e % 2, F:2 * F], w_up[e]).then_inc(gu_loaded[e % 2], 16)

            load_gu(0)
            load_gu(1)

            for w in range(3):
                for half in range(2):
                    f = Fill(2 * w + half)
                    act.wait_ge(pj_full, f.full)
                    nc.scalar.copy(w_hi[w][:, half * 512:half * 512 + 512], pj[f.bank][:, :]).then_inc(w_hi_ready, 1)

            def move(name, part, b, f, us):
                if name not in ("XT", "QK", "V", "X2T"):
                    return
                act.wait_ge(pj_full, f.full)
                if name == "XT":
                    nc.scalar.copy(xcT_hi[:, :], pj[f.bank][:, :]).then_inc(xcT_hi_ready, 1)
                elif name == "QK":
                    to = qk[us % 2][part % 2][:, part // 2 * 2:part // 2 * 2 + 2, :].rearrange("p c t -> p (c t)")
                    nc.scalar.copy(to, pj[f.bank][:, :]).then_inc(pj_moved[f.bank], 1)
                elif name == "V":
                    nc.scalar.copy(v[:, us % 2 * UB + part // 2, part % 2 * 8:part % 2 * 8 + 8, 0:HD],
                                   pj[f.bank][:, :].rearrange("p (h w) -> p h w", w=HD)).then_inc(pj_moved[f.bank], 1)
                elif name == "X2T":
                    if not (isinstance(b, int) and b == 0):
                        act.wait_ge(x2T_split, b)
                    nc.scalar.copy(x2T[:, :], pj[f.bank][:, 0:P]).then_inc(pj_moved[f.bank], 1)

            def exp_quad(n, c, par):
                act.wait_ge(shifted[c], n + 1)
                nc.scalar.activation(p_buf[:, c, par, :], p_buf[:, c, par, :], ACT.Exp, scale=SCALE)\
                  .then_inc(probs_ready[c], 1)

            def move_transposed(n, c, par, early=False):
                act.wait_ge(transposed[c], n + 1)
                if not early:
                    act.wait_ge(pv_done[c], n - 1)
                nc.scalar.copy(pT_buf[:, c, par, :], t_ps[c][:, :]).then_inc(probsT_ready[c], 1)

            move("XT", 0, None, prologue_fill("XT", 0), 0)
            for k in range(8):
                move("QK", k, None, prologue_fill("QK", k), 0)
            for k in range(4):
                move("V", k, None, prologue_fill("V", k), 0)
            exp_quad(0, 0, 0)
            exp_quad(0, 1, 0)
            for e in range(2, E):
                load_gu(e)

            def body(bd):
                for j in range(STEPS):
                    n, us = bd.octet(j), j // 4 + 1
                    for name, part, bb, f in bd.slot(j, "A"):
                        move(name, part, None if bb is None else bd.batch(bb), f, us)
                    for c in range(2):
                        move_transposed(n, c, j % 2, early=bd.first and j < 2)
                        if not (bd.last and j == STEPS - 1):
                            exp_quad(n + 1, c, (j + 1) % 2)
                    for s in "BC":
                        for name, part, bb, f in bd.slot(j, s):
                            move(name, part, None if bb is None else bd.batch(bb), f, us)

            body(FIRST)
            with act.Fori(1, NBODY - 1) as it:
                body(Body(it))
            body(LAST)
            move("X2T", 0, B - 2, Fill(TAIL), None)
            move("X2T", 0, B - 1, Fill(TAIL + 5), None)

            act.wait_ge(route, TOP_STEPS)
            nc.scalar.activation(gate_e[:, :, :], top[:, :, :], ACT.Exp, scale=-1.0).then_inc(gate_exp, 1)

            def group(g, first):
                for k in range(E * FC):
                    act.wait_ge(gu_done, E * FC * g + (k + 1))
                    if not (first and k < 2):
                        act.wait_ge(hid_ready, E * FC * g + (k - 1))
                    nc.scalar.activation(silu[k % 2], gate_ps[k % 2][:, :], ACT.Silu).then_inc(silu_done, 1)

            group(0, True)
            with act.Fori(1, NG) as g:
                group(g, False)

        @block.tensor
        def _(pe):
            def claim(f):
                if f.before is not None:
                    pe.wait_ge(pj_moved[f.bank], f.before)
                return pj[f.bank]

            pe.wait_ge(ident_ready, 1)
            for w in range(4):
                pe.wait_ge(w_loaded[w], 16)
                for half in range(2):
                    f = Fill(2 * w + half)
                    bank = claim(f)
                    for c in range(4):
                        mm = nc.tensor.transpose(bank[:, c * P:(c + 1) * P], w_stage[w][:, 4 * half + c, :], ident[:, :])
                    mm.then_inc(pj_full, 1)
            f = Fill(8)
            bank = claim(f)
            pe.wait_ge(small_loaded, 64)
            nc.tensor.transpose(bank[:, 0:E], rw_in[:, :], ident[0:E, 0:E]).then_inc(pj_full, 1)

            def product(outp, lhs, rhs):
                (lh, ll), (rh, rl) = lhs, rhs
                nc.tensor.matmul(outp, ll, rh, start=True, stop=False)
                nc.tensor.matmul(outp, lh, rl, start=False, stop=False)
                return nc.tensor.matmul(outp, lh, rh, start=False, stop=True)

            def fill(name, part, b, f, us, bd):
                bank = claim(f)
                if name == "XT":
                    u = us if bd is None else bd.unit(us)
                    pe.wait_ge(xn_ready, u + 1)
                    pe.wait_ge(c_loaded[us % 2], 16 * (0 if bd is None else bd.it) + 16 * (us // 2 + 1))
                    for i in range(UB):
                        mm = nc.tensor.transpose(bank[:, (UB + i) * P:(UB + i + 1) * P], c_in[us % 2][:, i, :], ident[:, :])
                    mm.then_inc(ctxT_taken, 1)
                    for i in range(UB):
                        mm = nc.tensor.transpose(bank[:, i * P:(i + 1) * P], xn[us % 2][:, i, :], ident[:, :])
                elif name == "QK":
                    if part == 0:
                        wait_moved(pe, [prologue_fill("XT", 0) if bd is None else bd.ahead("XT", 0, us)])
                    src = slice(0, UB * P) if part % 2 == 0 else slice(UB * P, 2 * UB * P)
                    for i in range(2):
                        c = part // 2 * 2 + i
                        w = part % 2
                        mm = product(bank[:, i * 256:i * 256 + 256],
                                     [t[:, c * P:(c + 1) * P] for t in (w_hi[w], w_lo[w])],
                                     [t[:, src] for t in (xcT_hi, xcT_lo)])
                elif name == "V":
                    tok = slice((UB + part // 2) * P, (UB + part // 2 + 1) * P)
                    feat = slice(part % 2 * 512, part % 2 * 512 + 512)
                    mm = product(bank[:, :], [t[:, tok] for t in (xcT_hi, xcT_lo)], [t[:, feat] for t in (w_hi[2], w_lo[2])])
                elif name == "OT":
                    if part == 0:
                        for c in range(2):
                            pe.wait_ge(o_ready[c], OB * b + OB)
                    for i in range(4):
                        c = 4 * part + i
                        mm = nc.tensor.transpose(bank[:, i * P:(i + 1) * P],
                                                 o_n[:, 2 * c:2 * c + 2, :].rearrange("p h w -> p (h w)"), ident[:, :])
                elif name == "OP":
                    for c in range(NCH):
                        mm = nc.tensor.matmul(bank[:, 0:P], oT[:, c * P:(c + 1) * P], woT[:, c, :],
                                              start=c == 0, stop=c == NCH - 1)
                elif name == "X2T":
                    pe.wait_ge(x2_ready, b + 1)
                    mm = nc.tensor.transpose(bank[:, 0:P], x2[:, :], ident[:, :])
                elif name == "LG":
                    mm = nc.tensor.matmul(bank[:, 0:E], x2T[:, :], rwT[:, :], start=True, stop=True)
                mm.then_inc(pj_full, 1)

            def scores(n, bs, o, us, needs, first=False):
                wait_moved(pe, needs)
                for c in range(2):
                    if not first:
                        pe.wait_ge(shifted[c], n)
                q, k = qk[us % 2]
                tok = slice(bs * P, (bs + 1) * P)
                for i in range(4):
                    for c in range(2):
                        rows = slice(c * HD, (c + 1) * HD)
                        mm = nc.tensor.matmul(s_ps[c][:, i * P:(i + 1) * P], q[rows, 4 * o + i, tok],
                                              k[rows, 4 * o + i, tok], start=True, stop=True)
                        if i == 3:
                            mm.then_inc(scored[c], 1)

            def transposes(n, par, first=False):
                for c in range(2):
                    pe.wait_ge(probs_ready[c], n + 1)
                    if not first:
                        pe.wait_ge(probsT_ready[c], n)
                    for i in range(4):
                        mm = nc.tensor.transpose(t_ps[c][:, i * P:(i + 1) * P], p_buf[:, c, par, i * P:(i + 1) * P],
                                                 ident[:, :])
                    mm.then_inc(transposed[c], 1)

            def values(n, slot, o, par, needs, first=False):
                wait_moved(pe, needs)
                for c in range(2):
                    pe.wait_ge(probsT_ready[c], n + 1)
                    if not first:
                        pe.wait_ge(o_ready[c], n)
                    for i in range(4):
                        mm = nc.tensor.matmul(o_ps[c][:, i * VW:(i + 1) * VW], pT_buf[:, c, par, i * P:(i + 1) * P],
                                              v[:, slot, 8 * o + 2 * i + c, :], start=True, stop=True)
                    mm.then_inc(pv_done[c], 1)

            wait_moved(pe, [Fill(k) for k in range(SETUP)])
            fill("XT", 0, None, prologue_fill("XT", 0), 0, None)
            for k in range(8):
                fill("QK", k, None, prologue_fill("QK", k), 0, None)
            for k in range(4):
                fill("V", k, None, prologue_fill("V", k), 0, None)
            pe.wait_ge(consts_ready, 3 + E)
            scores(0, 0, 0, 0, [prologue_fill("QK", k) for k in range(4)], first=True)

            def body(bd):
                for j in range(STEPS):
                    n = bd.octet(j)
                    if not (bd.last and j == STEPS - 1):
                        m = j + 1
                        o = m % OB
                        scores(n + 1, m // OB % UB, o, m // 4, [bd.ahead("QK", k, m // 4) for k in range(4 * o, 4 * o + 4)])

                    def run(s):
                        for name, part, bb, f in bd.slot(j, s):
                            if name == "OP":
                                wait_moved(pe, [bd.find("OT", h, [j - 1]) for h in range(2)])
                            if name == "LG":
                                wait_moved(pe, [bd.find("X2T", 0, [j])])
                            fill(name, part, None if bb is None else bd.batch(bb), f, j // 4 + 1, bd)

                    run("A")
                    transposes(n, j % 2, first=bd.first and j == 0)
                    run("B")
                    values(n, j // OB, j % OB, j % 2, [bd.ahead("V", 2 * (j // OB % UB) + j % OB, j // 4)],
                           first=bd.first and j == 0)
                    run("C")

            body(FIRST)
            with pe.Fori(1, NBODY - 1) as it:
                body(Body(it))
            body(LAST)
            fill("X2T", 0, B - 2, Fill(TAIL), None, None)
            fill("OT", 0, B - 1, Fill(TAIL + 1), None, None)
            fill("OT", 1, B - 1, Fill(TAIL + 2), None, None)
            wait_moved(pe, [Fill(TAIL)])
            fill("LG", 0, B - 2, Fill(TAIL + 3), None, None)
            wait_moved(pe, [Fill(TAIL + 1), Fill(TAIL + 2)])
            fill("OP", 0, B - 1, Fill(TAIL + 4), None, None)
            fill("X2T", 0, B - 1, Fill(TAIL + 5), None, None)
            wait_moved(pe, [Fill(TAIL + 5)])
            fill("LG", 0, B - 1, Fill(TAIL + 6), None, None)

            pe.wait_ge(gu_split, E)
            pe.wait_ge(wd_loaded, 16)
            pe.wait_ge(x2T_split, B)
            for c in range(2):
                pe.wait_ge(o_ready[c], NOCT)

            def gate_up(g, k, first):
                e, c = k // FC, k % FC
                if not (first and k < 2):
                    pe.wait_ge(hid_ready, E * FC * g + (k - 1))
                x2g = [t[:, bass.ds(g * (GT * P), GT * P)] for t in (x2T_hi, x2T_lo)]
                for bank, at in ((gate_ps[k % 2], c * P), (up_ps[k % 2], F + c * P)):
                    mm = product(bank[:, :], [t[:, e, at:at + P] for t in (wgu_hi, wgu_lo)], x2g)
                mm.then_inc(gu_done, 1)

            def down(g, e, first):
                pe.wait_ge(hid_ready, E * FC * g + FC * (e + 1))
                if not (first and e < 2):
                    pe.wait_ge(acc_done, E * g + (e - 1))
                for t in range(GT):
                    for c in range(FC):
                        mm = nc.tensor.matmul(y_ps[e % 2][:, t * P:(t + 1) * P], hid[e % 2][c][:, t * P:(t + 1) * P],
                                              wd[:, e, c, :], start=c == 0, stop=c == FC - 1)
                mm.then_inc(down_done, 1)

            def group(g, first):
                for k in range(E * FC):
                    gate_up(g, k, first)
                    if k % FC == FC - 1 and k >= FC:
                        down(g, k // FC - 1, first)
                down(g, E - 1, first)

            group(0, True)
            with pe.Fori(1, NG) as g:
                group(g, False)

        @block.vector
        def _(dve):
            dve.wait_ge(small_loaded, 64)
            dve.wait_ge(gates_ready, 1)
            nc.vector.tensor_scalar(bo_t[:, :], bo_b[:, :], tgates[:, 0:1], None, ALU.mult).then_inc(bias_ready, 1)

            def stats_x(u, par, arrived):
                dve.wait_ge(x_loaded[par], arrived)
                for i in range(UB):
                    op = nc.vector.bn_stats(st1[:, i, :], x_in[par][:, i, :])
                op.then_inc(stats1, 1)
                wait_apart(dve, stats1, u + 1)
                for i in range(UB):
                    nc.vector.bn_aggr(mv1[:, i, :], st1[:, i, :]).then_inc(agg1, 1)

            def norm_x(u, par):
                dve.wait_ge(rstd1, u + 1)
                for i in range(UB):
                    op = nc.vector.tensor_scalar(xn[par][:, i, :], x_in[par][:, i, :], mv1[:, i, 0:1],
                                                 rs1[:, i:i + 1], ALU.subtract, ALU.mult)
                op.then_inc(xn_ready, 1)

            def norm_x2(b):
                dve.wait_ge(rstd2, b + 1)
                nc.vector.tensor_scalar(x2[:, :], x1_all[:, bass.ds(b * P, P)], mv2[:, 0:1], rs2[:, :],
                                        ALU.subtract, ALU.mult).then_inc(x2_ready, 1)

            stats_x(0, 0, 16)
            norm_x(0, 0)
            stats_x(1, 1, 16)
            for w in range(3):
                for half in range(2):
                    f = Fill(2 * w + half)
                    at = slice(half * 512, half * 512 + 512)
                    dve.wait_ge(w_hi_ready, 2 * w + half + 1)
                    nc.vector.tensor_tensor(w_lo[w][:, at], pj[f.bank][:, :], w_hi[w][:, at].bitcast(F32), ALU.subtract)\
                      .then_inc(pj_moved[f.bank], 1)
            for half in range(2):
                f = Fill(6 + half)
                dve.wait_ge(pj_full, f.full)
                nc.vector.tensor_copy(woT[:, 4 * half:4 * half + 4, :].rearrange("p c d -> p (c d)"), pj[f.bank][:, :])\
                  .then_inc(pj_moved[f.bank], 1)
            f = Fill(8)
            dve.wait_ge(pj_full, f.full)
            nc.vector.tensor_copy(rwT[:, :], pj[f.bank][:, 0:E]).then_inc(pj_moved[f.bank], 1)
            norm_x(1, 1)

            def move(name, part, b, f, u):
                if name == "XT":
                    dve.wait_ge(xcT_hi_ready, u + 1)
                    nc.vector.tensor_tensor(xcT_lo[:, :], pj[f.bank][:, :], xcT_hi[:, :].bitcast(F32), ALU.subtract)\
                      .then_inc(pj_moved[f.bank], 1)
                elif name == "OT":
                    dve.wait_ge(pj_full, f.full)
                    nc.vector.tensor_copy(oT[:, part * 512:part * 512 + 512], pj[f.bank][:, :]).then_inc(pj_moved[f.bank], 1)
                elif name == "LG":
                    dve.wait_ge(pj_full, f.full)
                    nc.vector.tensor_copy(lg_all[:, bass.ds(b * E, E)], pj[f.bank][:, 0:E]).then_inc(pj_moved[f.bank], 1)
                elif name == "OP":
                    x1 = x1_all[:, bass.ds(b * P, P)]
                    dve.wait_ge(pj_full, f.full)
                    dve.wait_ge(xb_ready, b // UB + 1 if isinstance(b, int) else u + 1)
                    nc.vector.scalar_tensor_tensor(out=x1, in0=pj[f.bank][:, 0:P], scalar=tgates[:, 0:1], in1=x1,
                                                   op0=ALU.mult, op1=ALU.add).then_inc(pj_moved[f.bank], 1)
                    wait_apart(dve, pj_moved[f.bank], f.moved)
                    nc.vector.bn_stats(st2[:, :], x1).then_inc(stats2, 1)
                    wait_apart(dve, stats2, b + 1)
                    nc.vector.bn_aggr(mv2[:, :], st2[:, :]).then_inc(agg2, 1)

            def shift_quad(n, c, par, early=False):
                s = s_ps[c][:, :].rearrange("p (h k) -> p h k", h=4)
                dve.wait_ge(scored[c], n + 1)
                nc.vector.tensor_reduce(mx[c][:, :], s, AX.X, ALU.max).then_inc(max_ready[c], 1)
                dve.wait_ge(max_ready[c], n + 1)
                if not early:
                    dve.wait_ge(transposed[c], n - 1)
                nc.vector.tensor_tensor(p_buf[:, c, par, :].rearrange("p (h k) -> p h k", h=4), s,
                                        mx[c][:, :].unsqueeze(2).to_broadcast([P, 4, P]), ALU.subtract)\
                  .then_inc(shifted[c], 1)

            def normalize(n, c, o):
                pv = o_ps[c][:, 0:4 * VW].rearrange("p (h w) -> p h w", w=VW)
                dve.wait_ge(pv_done[c], n + 1)
                nc.vector.reciprocal(rden[c][:, :], pv[:, :, HD]).then_inc(rden_ready[c], 1)
                dve.wait_ge(rden_ready[c], n + 1)
                nc.vector.tensor_tensor(o_n[:, 8 * o + c:8 * o + 8:2, :], pv[:, :, 0:HD],
                                        rden[c][:, :].unsqueeze(2).to_broadcast([P, 4, HD]), ALU.mult)\
                  .then_inc(o_ready[c], 1)

            move("XT", 0, None, prologue_fill("XT", 0), 0)
            shift_quad(0, 0, 0, early=True)
            shift_quad(0, 1, 0, early=True)

            def body(bd):
                for j in range(STEPS):
                    n = bd.octet(j)
                    if not (bd.last and j == STEPS - 1):
                        for c in range(2):
                            shift_quad(n + 1, c, (j + 1) % 2, early=bd.first and j < 1)

                    if j % 4 == 3 and not bd.last:
                        norm_x(bd.unit(j // 4 + 2), j // 4)

                    def run(s):
                        for name, part, bb, f in bd.slot(j, s):
                            b = None if bb is None else bd.batch(bb)
                            u = bd.unit(j // 4 + 1) if bb is None else bd.unit(bb // UB)
                            move(name, part, b, f, u)

                    run("A")
                    run("B")
                    for c in range(2):
                        normalize(n, c, j % OB)
                    run("C")
                    if j % OB == 1 and not (bd.first and j < 2):
                        norm_x2(bd.batch(j // OB - 1))
                    if j % 4 == 2 and not bd.last:
                        us = j // 4
                        stats_x(bd.unit(us + 2), us, 16 * bd.it + 32)

            body(FIRST)
            with dve.Fori(1, NBODY - 1) as it:
                body(Body(it))
            body(LAST)
            move("OT", 0, B - 1, Fill(TAIL + 1), None)
            move("OT", 1, B - 1, Fill(TAIL + 2), None)
            move("LG", 0, B - 2, Fill(TAIL + 3), None)
            move("OP", 0, B - 1, Fill(TAIL + 4), None)
            norm_x2(B - 1)
            move("LG", 0, B - 1, Fill(TAIL + 6), None)

            steps = [0]

            def step(op):
                op.then_inc(route, 1)
                steps[0] += 1
                dve.wait_ge(route, steps[0])

            def over_experts(t):
                return t.unsqueeze(2).to_broadcast([P, B, E])

            dve.wait_ge(consts_ready, 3 + E)
            wait_moved(dve, [Fill(TAIL + 3), Fill(TAIL + 6)])
            lg = lg_all[:, :].rearrange("p (b e) -> p b e", e=E)
            for k in range(2):
                step(nc.vector.tensor_reduce(top[:, k, :], lg, AX.X, ALU.max))
                step(nc.vector.tensor_tensor(r_tmp, lg, over_experts(top[:, k, :]), ALU.is_equal))
                step(nc.vector.tensor_tensor(r_tmp, r_tmp, first_wins[:, :, :], ALU.mult))
                step(nc.vector.tensor_reduce(r_max[:, :], r_tmp, AX.X, ALU.max))
                step(nc.vector.tensor_tensor(one[k], r_tmp, over_experts(r_max[:, :]), ALU.is_equal))
                if k == 0:
                    step(nc.vector.scalar_tensor_tensor(out=lg, in0=one[0], scalar=-3e38, in1=lg,
                                                        op0=ALU.mult, op1=ALU.add))
            assert steps[0] == TOP_STEPS
            dve.wait_ge(gate_exp, 1)
            step(nc.vector.tensor_scalar(gate_e[:, :, :], gate_e[:, :, :], 1.0, None, ALU.add))
            step(nc.vector.reciprocal(gate_s[:, :, :], gate_e[:, :, :]))
            step(nc.vector.tensor_tensor(gate_n[:, :], gate_s[:, 0, :], gate_s[:, 1, :], ALU.add))
            step(nc.vector.tensor_scalar(gate_n[:, :], gate_n[:, :], 1e-10, None, ALU.add))
            step(nc.vector.reciprocal(r_max[:, :], gate_n[:, :]))
            step(nc.vector.tensor_scalar(r_max[:, :], r_max[:, :], tgates[:, 1:2], None, ALU.mult))
            step(nc.vector.tensor_tensor(gate_s[:, :, :], gate_s[:, :, :],
                                         r_max[:, :].unsqueeze(1).to_broadcast([P, 2, B]), ALU.mult))
            for k in range(2):
                step(nc.vector.tensor_tensor(one[k], one[k], over_experts(gate_s[:, k, :]), ALU.mult))
            step(nc.vector.tensor_tensor(ge_all, one[0], one[1], ALU.add))

            def hidden(g, k, first):
                e, c = k // FC, k % FC
                dve.wait_ge(silu_done, E * FC * g + (k + 1))
                if not (first and e < 2):
                    dve.wait_ge(down_done, E * g + (e - 1))
                nc.vector.tensor_tensor(hid[e % 2][c], silu[k % 2], up_ps[k % 2][:, :], ALU.mult).then_inc(hid_ready, 1)

            def add_expert(g, e, first):
                dve.wait_ge(down_done, E * g + (e + 1))
                if e > 0 or not first:
                    dve.wait_ge(acc_done, E * g + e)
                if e == E - 1 and not first:
                    dve.wait_ge(out_stored, 16 * g)
                for t in range(GT):
                    at = slice(t * P, (t + 1) * P)
                    so_far = x1_all[:, bass.ds(g * (GT * P) + t * P, P)] if e == 0 else acc[:, at]
                    to = out_sb if e == E - 1 else acc
                    op = nc.vector.scalar_tensor_tensor(out=to[:, at], in0=y_ps[e % 2][:, at],
                                                        scalar=ge_now[:, t * E + e:t * E + e + 1], in1=so_far,
                                                        op0=ALU.mult, op1=ALU.add)
                op.then_inc(acc_done, 1)

            def group(g, first):
                if not first:
                    dve.wait_ge(acc_done, E * g)
                nc.vector.tensor_copy(ge_now[:, :], ge_all.rearrange("p b e -> p (b e)")
                                      [:, bass.ds(g * (GT * E), GT * E)]).then_inc(ge_ready, 1)
                dve.wait_ge(ge_ready, g + 1)
                for k in range(E * FC):
                    hidden(g, k, first)
                    if k % FC == FC - 1 and k >= FC:
                        add_expert(g, k // FC - 1, first)
                add_expert(g, E - 1, first)

            group(0, True)
            with dve.Fori(1, NG) as g:
                group(g, False)


_INS = ["x", "ctx_1024", "g_xattn", "g_ffn", "L0_xattn_Wq", "L0_xattn_Wk", "L0_xattn_Wv", "L0_xattn_Wo", "L0_xattn_bo",
        "L0_ffn_router_w", "L0_ffn_w_gate", "L0_ffn_w_up", "L0_ffn_w_down"]


def kernel(**inputs):
    import numpy as _np
    import concourse.bacc as _bacc
    from concourse import mybir as _mybir
    from concourse.bass_utils import run_bass_kernel_spmd as _run

    nc = _bacc.Bacc("TRN2", target_bir_lowering=False, num_devices=1)
    arrays, args = {}, []
    for name in _INS:
        a = _np.ascontiguousarray(inputs[name])
        arrays[f"in_{name}"] = a
        args.append(nc.dram_tensor(f"in_{name}", a.shape, _mybir.dt.from_np(a.dtype), kind="ExternalInput").ap())
    args.append(nc.dram_tensor("out_0", (B, P, P), F32, kind="ExternalOutput").ap())
    build(nc, *args)
    r = _run(nc, [arrays], core_ids=[0])
    return r.results[0]["out_0"]
```

```python
from contextlib import ExitStack

import concourse.bass as bass
from concourse import mybir

F32 = mybir.dt.float32
F32R = mybir.dt.float32r
U32 = mybir.dt.uint32
I32 = mybir.dt.int32
ALU = mybir.AluOpType
ACT = mybir.ActivationFunctionType
AX = mybir.AxisListType

P = 128
B = 32
H, HD = 16, 64
NCH = H * HD // P
E, F = 8, 256
FC = F // P
EPS = 1e-5
ROOT_STEPS = 5
SCALE = 1.0 / HD ** 0.5

UB = 2
BU = 2
BB = UB * BU
OB = 2
STEPS = BB * OB
NBODY = B // BB
NOCT = B * OB
NUNIT = B // UB

K = 2
TOKENS = B * P
REGION = TOKENS + P
NOF = TOKENS // P
NT = TOKENS * K // P + E
RING = 8
BEHIND = 2
NTB = NT // RING
DEST, GATE, ROW = P, P + 1, P + 2
NOWHERE = K * TOKENS
assert NT % RING == 0

GT = 4
NG = B // GT
SPARE = E
PLAN_STEPS = 12
CONSTS = 17


def fills_at(j, first, last):
    q, bb, even = j % (UB * OB), j // OB, j % OB == 0
    slots = {"A": [], "B": [], "C": []}
    if not even and not (first and bb < 1):
        slots["A"].append(("X2T", 0, bb - 1))
    if not even and not (first and bb < 1):
        slots["B"].append(("LG", 0, bb - 1))
    due = {
        0: {"A": [("V", 1)], "B": [("V", 2), ("V", 3)], "C": [("V", 4), ("V", 5)]},
        1: {"A": [("V", 6)], "B": [("V", 7)]},
        2: {}, 3: {},
    }[q]
    ahead = {
        0: {},
        1: {"B": [("XT", 0)], "C": [("QK", 0)]},
        2: {"A": [("QK", 1)], "B": [("QK", 2), ("QK", 3)], "C": [("QK", 4)]},
        3: {"A": [("QK", 5)], "B": [("QK", 6), ("QK", 7)], "C": [("V", 0)]},
    }[q]
    for s, parts in due.items():
        slots[s] += [(name, part, None) for name, part in parts]
    if q == 3 and not (first and j < 4):
        slots["C"].append(("RK", 0, j // 4 - 1))
    if not (last and j >= UB * OB):
        for s, parts in ahead.items():
            slots[s] += [(name, part, None) for name, part in parts]
    return slots


def fills_of(first, last):
    return [(j, s, n) for j in range(STEPS) for s, parts in fills_at(j, first, last).items() for n, _ in enumerate(parts)]


PROLOGUE = [(name, part) for name, parts in
            [("WQ", 2), ("XT", 1), ("QK", 8), ("RW", 1), ("V", 1)] for part in range(parts)]
AHEAD = len(PROLOGUE)
N_FIRST = len(fills_of(True, False))
N_MID = len(fills_of(False, False))
N_LAST = len(fills_of(False, True))
assert N_MID % 2 == 0
BASE = AHEAD + N_FIRST - N_MID
TAIL = BASE + N_MID * (NBODY - 1) + N_LAST


class Fill:

    def __init__(self, fixed, it=0):
        self.bank = fixed % 2
        self.full = N_MID * it + (fixed + 1)
        self.moved = (N_MID // 2) * it + (fixed // 2 + 1)
        self.before = None if isinstance(it, int) and it == 0 and fixed < 2 else (N_MID // 2) * it + fixed // 2
        self.order = fixed


class Body:

    def __init__(self, it, first=False, last=False, second=False):
        self.it, self.first, self.last, self.second = it, first, last, second
        self.plan = fills_of(first, last)

    def slot(self, j, s):
        return [(name, part, bb, self.fill(self.plan.index((j, s, n))))
                for n, (name, part, bb) in enumerate(fills_at(j, self.first, self.last)[s])]

    def fill(self, at):
        return Fill(AHEAD + at) if self.first else Fill(BASE + at, self.it)

    def find(self, name, part, steps):
        for j in steps:
            kind = (False, False) if j < 0 else (self.first, self.last)
            for s, parts in fills_at(j % STEPS, *kind).items():
                for n, entry in enumerate(parts):
                    if entry[:2] == (name, part):
                        at = fills_of(*kind).index((j % STEPS, s, n))
                        return Fill(BASE - N_MID + at, self.it) if j < 0 else self.fill(at)

    def ahead(self, name, part, us):
        if us == 0 and self.first and not (name == "V" and part > 0):
            return prologue_fill(name, part)
        late = name == "V" and part > 0
        return self.find(name, part, range(4 * us, 4 * us + 2) if late else range(4 * us - 3, 4 * us))

    def octet(self, j):
        return STEPS * self.it + j

    def batch(self, bb):
        return BB * self.it + bb

    def unit(self, us):
        return BU * self.it + us

    def unit_of(self, name, part, j):
        return j // 4 if name == "V" and part > 0 else j // 4 + 1


def on_vector(when, part):
    return part % 2 == 1 if when is None else when in "AB"


def prologue_fill(name, part):
    return Fill(PROLOGUE.index((name, part)))


def build(nc, x, ctxt, g_xattn, g_ffn, Wq, Wk, Wv, Wo, bo, router_w, w_gate, w_up, w_down, out, sorted_rows, results):
    with ExitStack() as ctx:
        def sb(name, shape, dt=F32):
            return ctx.enter_context(nc.sbuf_tensor(name, shape, dt))

        def ps(name):
            return ctx.enter_context(nc.psum_tensor(name, [P, 512], F32))

        def sem(name):
            return ctx.enter_context(nc.semaphore(name))

        ident = sb("ident", [P, P])
        gates = sb("gates", [P, 2])
        tgates = sb("tgates", [P, 2])
        bo_b = sb("bo_b", [P, P])
        bo_t = sb("bo_t", [P, P])
        rw_in = sb("rw_in", [E, P])
        rwT = sb("rwT", [P, E])
        w_hi = [sb(f"w{c}_hi", [P, NCH * P], F32R) for c in "qk"]
        w_lo = [sb(f"w{c}_lo", [P, NCH * P], F32R) for c in "qk"]
        wvo_hi = sb("wvo_hi", [P, H * P], F32R)
        wvo_lo = sb("wvo_lo", [P, H * P], F32R)
        wgu_hi = sb("wgu_hi", [P, E, 2 * F], F32R)
        wgu_lo = sb("wgu_lo", [P, E, 2 * F], F32R)
        wd = sb("wd", [P, E, FC, P])
        x1_all = sb("x1_all", [P, B * P])
        gu_places = x1_all[:, :].rearrange("p (e f) -> p e f", e=E)
        gu_stage = [gu_places[:, 1 + (e if e < E - 1 else 1), :] for e in range(E)]
        x_in = [sb(f"x_in{i}", [P, UB, P]) for i in range(2)]
        c_in = [sb(f"c_in{i}", [P, UB, P]) for i in range(2)]
        xn = [sb(f"xn{i}", [P, UB, P]) for i in range(2)]
        st1 = sb("st1", [P, UB, 6])
        mv1 = sb("mv1", [P, UB, 2])
        ve1, rs1, nt1 = (sb(s, [P, UB]) for s in ("ve1", "rs1", "nt1"))
        xcT_hi = sb("xcT_hi", [P, 2 * UB * P], F32R)
        xcT_lo = sb("xcT_lo", [P, 2 * UB * P], F32R)
        qkT = sb("qkT", [P, 2, 2, NCH, UB * P])
        v = sb("v", [P, UB, H, P])
        woT = v[:, 1, 0:8, :]
        neg_max = [sb(f"neg_max{c}", [P, 4]) for c in "ab"]
        sums = [sb(f"sums{c}", [P, 4]) for c in "ab"]
        p_buf = sb("p_buf", [P, 2, 2, 512])
        pT_buf = sb("pT_buf", [P, 2, 2, 512])
        w_stage = [(p_buf, pT_buf)[w // 2][:, w % 2, :, :].rearrange("p a b -> p (a b)")
                   .rearrange("p (c d) -> p c d", c=NCH) for w in range(4)]
        rden = [sb(f"rden{c}", [P, 4]) for c in "ab"]
        st2 = sb("st2", [P, 6])
        mv2 = sb("mv2", [P, 2])
        minus_half = sb("minus_half", [P, UB])
        ve2, rs2, nt2 = (sb(s, [P, 1]) for s in ("ve2", "rs2", "nt2"))
        rows = sb("rows", [P, BB, K, ROW])
        x2T = sb("x2T", [P, P])
        iota_e = sb("iota_e", [P, E])
        before = sb("before", [P, P])
        ones = sb("ones", [P, P])
        dest = sb("dest", [P, B, K], U32)
        lg = sb("lg", [P, BB, E])
        topv = sb("topv", [P, BU, UB, 8])
        topi = sb("topi", [P, BU, UB, 8], U32)
        topf = sb("topf", [P, UB, K])
        chosen = sb("chosen", [P, BU, UB, K, E])
        count = sb("count", [P, UB, E])
        counted = sb("counted", [P, UB + 1, E])
        ranked = sb("ranked", [P, UB, K, E])
        slot = sb("slot", [P, BU, UB, K], U32)
        g_exp = sb("g_exp", [P, BU, UB, K])
        g_sig = sb("g_sig", [P, UB, K])
        g_sum = sb("g_sum", [P, UB])
        region_at = sb("region_at", [P, E])
        thresholds = sb("thresholds", [P, E, NOF])
        upto = sb("upto", [P, E, E])
        iota_t = sb("iota_t", [P, NT, E])
        row_t = sb("row_t", [P, NT])
        ends = sb("ends", [P, E])
        pads_at = sb("pads_at", [P, E], I32)
        tiles_tmp = sb("tiles_tmp", [P, E, NOF])
        tiles = sb("tiles", [P, E])
        tiles_tmp2 = sb("tiles_tmp2", [P, E, E])
        tiles_upto = sb("tiles_upto", [P, E])
        past = sb("past", [P, NT, E])
        tile_e = sb("tile_e", [P, NT])
        tile_before = sb("tile_before", [P, NT])
        expert_of = sb("expert_of", [P, BEHIND + NT], I32)
        first_row = sb("first_row", [P, NT], I32)
        pad_rows = sb("pad_rows", [P, E + SPARE, ROW])
        xt = sb("xt", [P, RING, ROW])
        xtT_hi = sb("xtT_hi", [P, 2, P], F32R)
        xtT_lo = sb("xtT_lo", [P, 2, P], F32R)
        silu = sb("silu", [P, 2, F])
        hid = sb("hid", [P, 2, F])
        hidT = sb("hidT", [P, 2, F])
        y = sb("y", [P, RING, P])
        y12 = qkT[:, :, :, :, :].rearrange("p i w c t -> p (i w c t)")\
            .rearrange("p (g k d) -> p g k d", g=NG, k=K)

        s_ps = [ps("sa"), ps("sb")]
        t_ps = [ps("ta"), ps("tb")]
        o_ps = [ps("oa"), ps("ob")]
        pj = [ps("pj0"), ps("pj1")]
        wk_ps, wo_ps, vo_ps = s_ps, t_ps, o_ps
        gu_ps, xt_ps, ht_ps, y_ps = s_ps, t_ps, o_ps, pj

        w_loaded = [sem(f"w{c}_loaded") for c in "qkvo"]
        small_loaded = sem("small_loaded")
        gates_ready = sem("gates_ready")
        bias_ready = sem("bias_ready")
        ident_ready = sem("ident_ready")
        consts_ready = sem("consts_ready")
        gu_loaded = [sem(f"gu_loaded{e}") for e in range(E)]
        gu_split = sem("gu_split")
        gu_hi_done = sem("gu_hi_done")
        wd_loaded = sem("wd_loaded")
        x_loaded = [sem(f"x_loaded{i}") for i in range(2)]
        c_loaded = [sem(f"c_loaded{i}") for i in range(2)]
        stats1, agg1, rstd1, xn_ready = (sem(s) for s in ("stats1", "agg1", "rstd1", "xn_ready"))
        root1, root2 = sem("root1"), sem("root2")
        xb_ready = sem("xb_ready")
        ctxT_taken = sem("ctxT_taken")
        pj_full = sem("pj_full")
        pj_moved = [sem(f"pj_moved{i}") for i in range(2)]
        w_hi_ready = sem("w_hi_ready")
        w_full, w_moved = sem("w_full"), sem("w_moved")
        xcT_hi_ready = sem("xcT_hi_ready")
        scored = [sem(f"scored{c}") for c in "ab"]
        max_ready = [sem(f"max_ready{c}") for c in "ab"]
        exp_ready = [sem(f"exp_ready{c}") for c in "ab"]
        probs_ready = [sem(f"probs_ready{c}") for c in "ab"]
        transposed = [sem(f"transposed{c}") for c in "ab"]
        probsT_ready = [sem(f"probsT_ready{c}") for c in "ab"]
        pv_done = [sem(f"pv_done{c}") for c in "ab"]
        rden_ready = [sem(f"rden_ready{c}") for c in "ab"]
        x1_ready, stats2, agg2, rstd2, x2_ready = (sem(s) for s in ("x1_ready", "stats2", "agg2", "rstd2", "x2_ready"))
        top_ready, topi_ready, topf_ready, chosen_ready = (
            sem(n) for n in ("top_ready", "topi_ready", "topf_ready", "chosen_ready"))
        count_chain, counted_ready = sem("count_chain"), sem("counted_ready")
        last_count = sem("last_count")
        slots_ready = sem("slots_ready")
        gate_exp, gate_chain, gates_done = sem("gate_exp"), sem("gate_chain"), sem("gates_done")
        dest_ready = sem("dest_ready")
        scattered = [sem(f"scattered{i}") for i in range(BU)]
        spare_written = sem("spare_written")
        pads_written = sem("pads_written")
        plan = sem("plan")
        xt_loaded = [sem(f"xt_loaded{i}") for i in range(RING)]
        xt_turned, xt_hi_ready, xt_ready = sem("xt_turned"), sem("xt_hi_ready"), sem("xt_ready")
        table_in = sem("table_in")
        gu_done, silu_ready, hid_ready = sem("gu_done"), sem("silu_ready"), sem("hid_ready")
        hid_turned, hidT_ready, down_done = sem("hid_turned"), sem("hidT_ready"), sem("down_done")
        y_ready = sem("y_ready")
        y_scattered = [sem(f"y_scattered{i}") for i in range(RING)]
        y12_loaded = [sem(f"y12_loaded{i}") for i in range(NG)]
        part_ready, total_ready = sem("part_ready"), sem("total_ready")
        out_stored = sem("out_stored")
        passed = sem("passed")

        block = ctx.enter_context(nc.Block())

        def load_values(table, engine, most):
            return nc.values_load_multi_w_load_instructions(
                table, engines=[engine], min_val=0, max_val=most,
                skip_runtime_bounds_check_because="the tables' entries are clamped where they are made")[1]

        def projected(name, part, us):
            if name == "QK":
                return qkT[:, us % 2, part % 2, part // 2 * 2:part // 2 * 2 + 2, :].rearrange("p c t -> p (c t)")
            return v[:, part // 4, part % 4 * 4:part % 4 * 4 + 4, :].rearrange("p h d -> p (h d)")

        def wait_moved(eng, fills):
            for bank in range(2):
                of = [f for f in fills if f.bank == bank]
                if of:
                    eng.wait_ge(pj_moved[bank], max(of, key=lambda f: f.order).moved)

        def wait_apart(eng, waited, value):
            eng.wait_ge(waited, value)
            eng.sem_inc(passed, 1)

        FIRST, SECOND, LAST = Body(0, first=True), Body(1, second=True), Body(NBODY - 1, last=True)

        @block.sync
        def _(sp):
            def load(u, par):
                sp.dma_start(x_in[par][:, :, :], x[bass.ds(u * UB, UB)].rearrange("b t d -> t b d"))\
                  .then_inc(x_loaded[par], 16)
                sp.dma_start(c_in[par][:, :, :], ctxt[bass.ds(u * UB, UB)].rearrange("b t d -> t b d"))\
                  .then_inc(c_loaded[par], 16)

            load(0, 0)
            sp.dma_start(w_stage[0], Wq.rearrange("(c p) d -> p c d", p=P)).then_inc(w_loaded[0], 16)
            sp.dma_start(w_stage[1], Wk.rearrange("(c p) d -> p c d", p=P)).then_inc(w_loaded[1], 16)
            sp.dma_start(w_stage[3], Wo.rearrange("p (c d) -> p c d", d=P)).then_inc(w_loaded[3], 16)
            sp.dma_start(w_stage[2], Wv.rearrange("(c p) d -> p c d", p=P)).then_inc(w_loaded[2], 16)
            load(1, 1)
            for e in range(E):
                if e == E - 1:
                    sp.dma_start(wd[:, :, :, :], w_down.rearrange("e (c p) d -> p e c d", p=P)).then_inc(wd_loaded, 16)
                    sp.wait_ge(gu_split, 2)
                sp.dma_start(gu_stage[e][:, 0:F], w_gate[e]).then_inc(gu_loaded[e], 16)
                sp.dma_start(gu_stage[e][:, F:2 * F], w_up[e]).then_inc(gu_loaded[e], 16)
            with sp.Fori(1, NUNIT // 2) as i:
                for par in range(2):
                    sp.wait_ge(xn_ready, 2 * i + (par - 1))
                    sp.wait_ge(xb_ready, 2 * i + (par - 1))
                    sp.wait_ge(ctxT_taken, 2 * i + (par - 1))
                    load(2 * i + par, par)
            sp.wait_ge(consts_ready, CONSTS)
            sp.dma_start(sorted_rows[E * REGION:E * REGION + SPARE * P].rearrange("(n p) w -> p n w", p=P),
                         pad_rows[:, E:E + SPARE, :]).then_inc(spare_written, 16)

            sp.wait_ge(plan, 1)
            ends_at = load_values(pads_at[0:1, :], mybir.EngineType.SP, E * REGION)
            for e in range(E):
                sp.dma_start(sorted_rows[bass.ds(ends_at[e], P), :], pad_rows[:, e, :]).then_inc(pads_written, 16)
            sp.wait_ge(plan, PLAN_STEPS)
            for us in range(BU):
                sp.wait_ge(scattered[us], 16 * UB * K * NUNIT // BU)
            sp.wait_ge(pads_written, 16 * E)
            sp.wait_ge(spare_written, 16)

            def load_tiles(it, first=False):
                starts = load_values(first_row[0:1, bass.ds(it * RING, RING)], mybir.EngineType.SP,
                                     E * REGION + (SPARE - 1) * P)
                for r in range(RING):
                    if not first:
                        sp.wait_ge(y_scattered[r], 16 * it)
                    sp.dma_start(xt[:, r, :], sorted_rows[bass.ds(starts[r], P), :]).then_inc(xt_loaded[r], 16)

            load_tiles(0, first=True)
            with sp.Fori(1, NTB) as it:
                load_tiles(it)

            for r in range(RING):
                sp.wait_ge(y_scattered[r], 16 * NTB)
            both = results[0:K * TOKENS].rearrange("(k b t) d -> t k b d", k=K, t=P)

            for g in range(NG):
                for k in range(K):
                    sp.dma_start(y12[:, g, k, :].rearrange("p (b d) -> p b d", d=P),
                                 both[:, k, g * GT:(g + 1) * GT, :]).then_inc(y12_loaded[g], 16)
            for g in range(NG):
                sp.wait_ge(total_ready, g + 1)
                sp.dma_start(out[g * GT:(g + 1) * GT].rearrange("b t d -> t b d"),
                             y12[:, g, 1, :].rearrange("p (b d) -> p b d", b=GT)).then_inc(out_stored, 16)
            sp.wait_ge(out_stored, 16 * NG)

        @block.gpsimd
        def _(pool):
            nc.gpsimd.memset(ident[:, :], 0.0).then_inc(consts_ready, 1)
            pool.wait_ge(consts_ready, 1)
            nc.gpsimd.affine_select(out=ident[:, :], in_=ident[:, :], compare_op=ALU.not_equal, fill=1.0,
                                    base=0, pattern=[[-1, P]], channel_multiplier=1).then_inc(ident_ready, 1)
            nc.gpsimd.memset(minus_half[:, :], -0.5).then_inc(consts_ready, 1)

            def inverse_root(k, n, counted, agg, chain, done, var, ve, rs, nt):
                at = [0]

                def step(op, last=False):
                    if last:
                        return op.then_inc(done, 1)
                    op.then_inc(chain, 1)
                    at[0] += 1
                    wait_apart(pool, chain, ROOT_STEPS * k + at[0])

                wait_apart(pool, agg, counted)
                step(nc.gpsimd.tensor_scalar(ve, var, EPS, None, ALU.add))
                step(nc.gpsimd.tensor_tensor(rs, ve, minus_half[:, 0:n], ALU.pow))
                step(nc.gpsimd.tensor_tensor(nt, ve, rs, ALU.mult))
                step(nc.gpsimd.tensor_tensor(nt, nt, rs, ALU.mult))
                step(nc.gpsimd.tensor_scalar(nt, nt, -0.5, 1.5, ALU.mult, ALU.add))
                step(nc.gpsimd.tensor_tensor(rs, rs, nt, ALU.mult), last=True)

            def root_x(u):
                inverse_root(u, UB, UB * (u + 1), agg1, root1, rstd1, mv1[:, :, 1], ve1[:, :], rs1[:, :], nt1[:, :])

            def root_x2(b):
                inverse_root(b, 1, b + 1, agg2, root2, rstd2, mv2[:, 1:2], ve2[:, :], rs2[:, :], nt2[:, :])

            pool.wait_ge(consts_ready, 2)
            root_x(0)
            nc.gpsimd.memset(ones[:, :], 1.0).then_inc(consts_ready, 1)
            nc.gpsimd.memset(before[:, :], 1.0).then_inc(consts_ready, 1)
            nc.gpsimd.memset(upto[:, :, :], 1.0).then_inc(consts_ready, 1)
            nc.gpsimd.memset(pad_rows[:, :, :], 0.0).then_inc(consts_ready, 1)
            nc.gpsimd.memset(expert_of[:, 0:BEHIND], 0).then_inc(consts_ready, 1)

            def iota(t, pattern, channel=0):
                nc.gpsimd.iota(t, pattern, base=0, channel_multiplier=channel,
                               allow_small_or_imprecise_dtypes=True).then_inc(consts_ready, 1)

            iota(iota_e[:, :], [[1, E]])
            iota(dest[:, :, :], [[P, B], [TOKENS, K]], 1)
            iota(region_at[:, :], [[REGION, E]])
            iota(thresholds[:, :, :], [[0, E], [P, NOF]])
            iota(iota_t[:, :, :], [[1, NT], [0, E]])
            iota(row_t[:, :], [[P, NT]])
            iota(counted[:, UB, :], [[REGION // P, E]])
            pool.wait_ge(consts_ready, CONSTS - 3)
            nc.gpsimd.affine_select(out=before[:, :], in_=before[:, :], compare_op=ALU.is_gt, fill=0.0,
                                    base=0, pattern=[[1, P]], channel_multiplier=-1).then_inc(consts_ready, 1)
            nc.gpsimd.affine_select(out=upto[:, :, :], in_=upto[:, :, :], compare_op=ALU.is_ge, fill=0.0,
                                    base=0, pattern=[[1, E], [-1, E]], channel_multiplier=0).then_inc(consts_ready, 1)
            nc.gpsimd.iota(pad_rows[:, :, DEST].bitcast(U32), [[P, E + SPARE]], base=NOWHERE, channel_multiplier=1)\
              .then_inc(consts_ready, 1)

            def residual(u, par, arrived):
                pool.wait_ge(x_loaded[par], arrived)
                nc.gpsimd.tensor_tensor(x1_all[:, bass.ds(u * (UB * P), UB * P)].rearrange("p (b d) -> p b d", b=UB),
                                        x_in[par][:, :, :], bo_t[:, :].unsqueeze(1).to_broadcast([P, UB, P]),
                                        ALU.add).then_inc(xb_ready, 1)

            def count_unit(u, us):
                pool.wait_ge(chosen_ready, u + 1)
                if not (isinstance(u, int) and u == 0):
                    pool.wait_ge(slots_ready, u)
                nc.gpsimd.tensor_tensor(count[:, :, :], chosen[:, us, :, 0, :], chosen[:, us, :, 1, :], ALU.add)\
                  .then_inc(count_chain, 1)
                nc.gpsimd.tensor_copy(counted[:, 0, :], counted[:, UB, :]).then_inc(count_chain, 1)
                for b in range(UB):
                    pool.wait_ge(count_chain, (UB + 1) * u + (2 + b))
                    nc.gpsimd.tensor_tensor(counted[:, b + 1, :], counted[:, b, :], count[:, b, :], ALU.add)\
                      .then_inc(count_chain if b < UB - 1 else counted_ready, 1)

            def scatter_unit(u, us, earlier):
                if earlier is not None:
                    wait_apart(pool, scattered[us], earlier)
                nc.gpsimd.tensor_copy(rows[:, us * UB:(us + 1) * UB, :, DEST].bitcast(U32),
                                      dest[:, bass.ds(u * UB, UB), :]).then_inc(dest_ready, 1)
                pool.wait_ge(dest_ready, u + 1)
                pool.wait_ge(gates_done, u + 1)
                pool.wait_ge(x2_ready, UB * (u + 1))
                wait_apart(pool, slots_ready, u + 1)
                for b in range(UB):
                    for k in range(K):
                        nc.gpsimd.indirect_dma_start(
                            sorted_rows, bass.IndirectOffsetOnAxis(slot[:, us, b, k:k + 1], axis=0),
                            rows[:, us * UB + b, k, :], None).then_inc(scattered[us], 16)

            pool.wait_ge(consts_ready, CONSTS)
            root_x(1)
            pool.wait_ge(bias_ready, 1)
            residual(0, 0, 16)
            residual(1, 1, 16)
            for e in range(E):
                pool.wait_ge(gu_loaded[e], 32)
                nc.gpsimd.tensor_copy(wgu_hi[:, e, :], gu_stage[e]).then_inc(gu_hi_done, 1)
                pool.wait_ge(gu_hi_done, e + 1)
                nc.gpsimd.tensor_tensor(wgu_lo[:, e, :], gu_stage[e], wgu_hi[:, e, :].bitcast(F32),
                                        ALU.subtract).then_inc(gu_split, 1)

            def body(bd):
                for j in range(STEPS):
                    if j % OB == 0 and not (bd.first and j == 0):
                        root_x2(bd.batch(j // OB - 1))
                    if j % 4 == 2 and not (bd.first and j < 4):
                        count_unit(bd.unit(j // 4 - 1), (j // 4 + 1) % BU)
                    if j % 4 == 2 and not bd.last:
                        residual(bd.unit(j // 4 + 2), j // 4, 16 * bd.it + 32)
                    if j % 4 == 0 and not bd.last:
                        root_x(bd.unit(j // 4 + 2))
                    if j % 4 == 3:
                        us = j // 4
                        ru = bd.unit(us - 1)
                        if bd.last and us == BU - 1:
                            root_x2(B - 1)
                        if not (bd.first and us == 0):
                            scatter_unit(ru, (us + 1) % BU, None if bd.first or (bd.second and us == 0) else
                                         16 * UB * K * (bd.it + (us - 1)))

            body(FIRST)
            body(SECOND)
            with pool.Fori(2, NBODY - 1) as it:
                body(Body(it))
            body(LAST)
            scatter_unit(NUNIT - 1, BU - 1, 16 * UB * K * (NBODY - 1))
            def scatter_results(it):
                for r in range(RING):
                    wait_apart(pool, y_ready, RING * it + (r + 1))
                    nc.gpsimd.indirect_dma_start(results, bass.IndirectOffsetOnAxis(xt[:, r, DEST:DEST + 1].bitcast(U32), axis=0),
                                                 y[:, r, :], None)\
                      .then_inc(y_scattered[r], 16)

            with pool.Fori(0, NTB) as it:
                scatter_results(it)

        @block.scalar
        def _(act):
            act.dma_start(gates[:, 0:1], g_xattn.partition_broadcast(P)).then_inc(small_loaded, 16)
            act.dma_start(gates[:, 1:2], g_ffn.partition_broadcast(P)).then_inc(small_loaded, 16)
            act.dma_start(bo_b[:, :], bo.partition_broadcast(P)).then_inc(small_loaded, 16)
            act.dma_start(rw_in[:, :], router_w).then_inc(small_loaded, 16)

            def high_weights(w, half):
                if w == 0:
                    f = prologue_fill("WQ", half)
                    act.wait_ge(pj_full, f.full)
                    bank = pj[f.bank]
                else:
                    act.wait_ge(w_full, half + 1)
                    bank = wk_ps[half]
                nc.scalar.copy(w_hi[w][:, half * 512:half * 512 + 512], bank[:, :]).then_inc(w_hi_ready, 1)

            def high_values(part):
                act.wait_ge(w_full, 4 + part + 1)
                nc.scalar.copy(wvo_hi[:, part * 512:part * 512 + 512], vo_ps[part % 2][:, :]).then_inc(w_hi_ready, 1)

            def move(name, part, f, us, when=None):
                if name not in ("XT", "QK", "V", "X2T") or name in ("QK", "V") and on_vector(when, part):
                    return
                act.wait_ge(pj_full, f.full)
                if name == "XT":
                    nc.scalar.copy(xcT_hi[:, :], pj[f.bank][:, :]).then_inc(xcT_hi_ready, 1)
                elif name == "QK" and part % 2 == 0:
                    nc.scalar.activation(projected(name, part, us), pj[f.bank][:, :], ACT.Copy, scale=SCALE)\
                      .then_inc(pj_moved[f.bank], 1)
                elif name in ("QK", "V"):
                    nc.scalar.copy(projected(name, part, us), pj[f.bank][:, :]).then_inc(pj_moved[f.bank], 1)
                elif name == "X2T":
                    nc.scalar.copy(x2T[:, :], pj[f.bank][:, 0:P]).then_inc(pj_moved[f.bank], 1)

            def exp_quad(n, c, par, early=False):
                if not early:
                    act.wait_ge(transposed[c], n - 1)
                    act.wait_ge(probs_ready[c], n)
                act.wait_ge(max_ready[c], n + 1)
                for i in range(4):
                    op = nc.scalar.activation(p_buf[:, c, par, i * P:(i + 1) * P], s_ps[c][:, i * P:(i + 1) * P], ACT.Exp,
                                              bias=neg_max[c][:, i:i + 1], scale=1.0, accum_out=sums[c][:, i:i + 1])
                op.then_inc(exp_ready[c], 1)

            def move_transposed(n, c, par, early=False):
                act.wait_ge(transposed[c], n + 1)
                if not early:
                    act.wait_ge(pv_done[c], n - 1)
                nc.scalar.copy(pT_buf[:, c, par, :], t_ps[c][:, :]).then_inc(probsT_ready[c], 1)

            def gate_exps(u, us):
                act.wait_ge(chosen_ready, u + 1)
                nc.scalar.activation(g_exp[:, us, :, :], topv[:, us, :, 0:K], ACT.Exp, scale=-1.0).then_inc(gate_exp, 1)

            for half in range(2):
                high_weights(0, half)
            move("XT", 0, prologue_fill("XT", 0), 0)
            for half in range(2):
                high_weights(1, half)
            act.wait_ge(small_loaded, 64)
            nc.scalar.activation(tgates[:, :], gates[:, :], ACT.Tanh).then_inc(gates_ready, 1)
            for k in range(4):
                move("QK", k, prologue_fill("QK", k), 0)
            for c in range(2):
                exp_quad(0, c, 0, early=True)
                high_values(2 * c)
                high_values(2 * c + 1)
                for k in range(2):
                    move("QK", 4 + 2 * c + k, prologue_fill("QK", 4 + 2 * c + k), 0)
            move("V", 0, prologue_fill("V", 0), 0)

            def body(bd):
                for j in range(STEPS):
                    n = bd.octet(j)
                    more = not (bd.last and j == STEPS - 1)

                    def run(s):
                        for name, part, _, f in bd.slot(j, s):
                            move(name, part, f, bd.unit_of(name, part, j), s)

                    run("A")
                    if more:
                        exp_quad(n + 1, 0, (j + 1) % 2, early=bd.first and j == 0)
                    for c in range(2):
                        move_transposed(n, c, j % 2, early=bd.first and j < 2)
                    run("B")
                    if more:
                        exp_quad(n + 1, 1, (j + 1) % 2, early=bd.first and j == 0)
                    run("C")
                    if j % 4 == 2 and not (bd.first and j < 4):
                        gate_exps(bd.unit(j // 4 - 1), (j // 4 + 1) % BU)

            body(FIRST)
            with act.Fori(1, NBODY - 1) as it:
                body(Body(it))
            body(LAST)
            move("X2T", 0, Fill(TAIL), None)
            gate_exps(NUNIT - 1, BU - 1)
            nc.scalar.activation(silu[:, 0, 0:1], tgates[:, 0:1], ACT.Silu).then_inc(table_in, 1)

            def high(t, r):
                act.wait_ge(xt_turned, t + 1)
                if not (isinstance(t, int) and t < 2):
                    act.wait_ge(gu_done, t - 1)
                nc.scalar.copy(xtT_hi[:, r % 2, :], xt_ps[r % 2][:, 0:P]).then_inc(xt_hi_ready, 1)

            def gate(t, r):
                act.wait_ge(gu_done, t + 1)
                if isinstance(t, int) and t == 0:
                    act.wait_ge(table_in, 1)
                if not (isinstance(t, int) and t < 2):
                    act.wait_ge(hid_ready, t - 1)
                nc.scalar.activation(silu[:, r % 2, :], gu_ps[r % 2][:, 0:F], ACT.Silu).then_inc(silu_ready, 1)

            def move_hidden(t, r):
                act.wait_ge(hid_turned, t + 1)
                if not (isinstance(t, int) and t < 2):
                    act.wait_ge(down_done, t - 1)
                nc.scalar.copy(hidT[:, r % 2, :], ht_ps[r % 2][:, 0:F]).then_inc(hidT_ready, 1)

            def tiles_body(it, first=False, last=False):
                for r in range(RING):
                    t = RING * it + r
                    if not (last and r == RING - 1):
                        high(t + 1, r + 1)
                    gate(t, r)
                    if not (first and r == 0):
                        move_hidden(t - 1, r - 1)

            high(0, 0)
            tiles_body(0, first=True)
            with act.Fori(1, NTB - 1) as it:
                tiles_body(it)
            tiles_body(NTB - 1, last=True)
            move_hidden(NT - 1, NT - 1)

        @block.tensor
        def _(pe):
            def claim(f):
                if f.before is not None:
                    pe.wait_ge(pj_moved[f.bank], f.before)
                return pj[f.bank]

            pe.wait_ge(ident_ready, 1)

            def turn_weights(w, bank_of, done):
                pe.wait_ge(w_loaded[w], 16)
                for half in range(2):
                    bank = bank_of(half)
                    for c in range(4):
                        mm = nc.tensor.transpose(bank[:, c * P:(c + 1) * P], w_stage[w][:, 4 * half + c, :], ident[:, :])
                    mm.then_inc(done, 1)

            def value_weights(part):
                pe.wait_ge(w_moved, 4 if part < 2 else 4 + part - 1)
                for i in range(4):
                    c, row = part // 2 * 4 + i, slice(part % 2 * HD, (part % 2 + 1) * HD)
                    mm = nc.tensor.matmul(vo_ps[part % 2][:, i * P:(i + 1) * P], w_stage[2][row, c, :], woT[row, c, :],
                                          start=True, stop=True)
                mm.then_inc(w_full, 1)

            def product(outp, lhs, rhs):
                (lh, ll), (rh, rl) = lhs, rhs
                nc.tensor.matmul(outp, ll, rh, start=True, stop=False)
                nc.tensor.matmul(outp, lh, rl, start=False, stop=False)
                return nc.tensor.matmul(outp, lh, rh, start=False, stop=True)

            def so_far():
                return counted[:, UB, :].unsqueeze(1).to_broadcast([P, UB, E])

            def fill(name, part, b, f, us, bd):
                bank = claim(f)
                if name == "XT":
                    u = us if bd is None else bd.unit(us)
                    pe.wait_ge(xn_ready, u + 1)
                    pe.wait_ge(c_loaded[us % 2], 16 * (0 if bd is None else bd.it) + 16 * (us // 2 + 1))
                    for i in range(UB):
                        mm = nc.tensor.transpose(bank[:, (UB + i) * P:(UB + i + 1) * P], c_in[us % 2][:, i, :], ident[:, :])
                    mm.then_inc(ctxT_taken, 1)
                    for i in range(UB):
                        mm = nc.tensor.transpose(bank[:, i * P:(i + 1) * P], xn[us % 2][:, i, :], ident[:, :])
                elif name == "QK":
                    if part == 0:
                        wait_moved(pe, [prologue_fill("XT", 0) if bd is None else bd.ahead("XT", 0, us)])
                    src = slice(0, UB * P) if part % 2 == 0 else slice(UB * P, 2 * UB * P)
                    for i in range(2):
                        c = part // 2 * 2 + i
                        w = part % 2
                        mm = product(bank[:, i * 256:i * 256 + 256],
                                     [t[:, c * P:(c + 1) * P] for t in (w_hi[w], w_lo[w])],
                                     [t[:, src] for t in (xcT_hi, xcT_lo)])
                elif name == "V":
                    tok = slice((UB + part // 4) * P, (UB + part // 4 + 1) * P)
                    feat = slice(part % 4 * 512, part % 4 * 512 + 512)
                    mm = product(bank[:, :], [t[:, tok] for t in (xcT_hi, xcT_lo)], [t[:, feat] for t in (wvo_hi, wvo_lo)])
                elif name == "X2T":
                    pe.wait_ge(x2_ready, b + 1)
                    mm = nc.tensor.transpose(bank[:, 0:P], rows[:, us % BB, 0, 0:P], ident[:, :])
                elif name == "LG":
                    mm = nc.tensor.matmul(bank[:, 0:E], x2T[:, :], rwT[:, :], start=True, stop=True)
                elif name == "RK":
                    pe.wait_ge(counted_ready, b + 1)
                    nc.tensor.matmul(bank[:, 0:UB * E], before[:, :], count[:, :, :].rearrange("p b e -> p (b e)"),
                                     start=True, stop=False)
                    mm = nc.tensor.matmul(bank[:, 0:UB * E], ones[:, :],
                                          counted[:, 0:UB, :].rearrange("p b e -> p (b e)"), start=False, stop=True)
                elif name == "LAST RK":
                    pe.wait_ge(last_count, 1)
                    nc.tensor.matmul(bank[:, 0:UB * E], before[:, :], count[:, :, :].rearrange("p b e -> p (b e)"),
                                     start=True, stop=False)
                    nc.tensor.matmul(bank[:, E:UB * E], ones[:, :], count[:, 0, :], start=False, stop=False)
                    mm = nc.tensor.matmul(bank[:, 0:UB * E], ones[:, :], so_far(), start=False, stop=True)
                elif name == "CT":
                    for i in range(UB):
                        nc.tensor.matmul(bank[:, 0:E], ones[:, :], count[:, i, :], start=i == 0, stop=False)
                    mm = nc.tensor.matmul(bank[:, 0:E], ones[:, :], counted[:, UB, :], start=False, stop=True)
                mm.then_inc(pj_full, 1)

            def scores(n, bs, o, us, needs, first=False):
                wait_moved(pe, needs)
                for c in range(2):
                    if not first:
                        pe.wait_ge(exp_ready[c], n)
                q, k = (qkT[:, us % 2, w, :, :] for w in range(2))
                tok = slice(bs * P, (bs + 1) * P)
                for i in range(4):
                    for c in range(2):
                        rows = slice(c * HD, (c + 1) * HD)
                        mm = nc.tensor.matmul(s_ps[c][:, i * P:(i + 1) * P], q[rows, 4 * o + i, tok],
                                              k[rows, 4 * o + i, tok], start=True, stop=True)
                        if i == 3:
                            mm.then_inc(scored[c], 1)

            def transposes(n, par, first=False):
                for c in range(2):
                    pe.wait_ge(probs_ready[c], n + 1)
                    if not first:
                        pe.wait_ge(probsT_ready[c], n)
                    for i in range(4):
                        mm = nc.tensor.transpose(t_ps[c][:, i * P:(i + 1) * P], p_buf[:, c, par, i * P:(i + 1) * P],
                                                 ident[:, :])
                    mm.then_inc(transposed[c], 1)

            def values(n, b, slot, o, par, needs, early=False):
                wait_moved(pe, needs)
                if o == 0 and not early:
                    pe.wait_ge(x1_ready, b - 1)
                for c in range(2):
                    pe.wait_ge(probsT_ready[c], n + 1)
                    for i in range(4):
                        mm = nc.tensor.matmul(o_ps[slot][:, 0:P], pT_buf[:, c, par, i * P:(i + 1) * P],
                                              v[:, slot, 8 * o + 4 * c + i, :], start=o == 0 and c == 0 and i == 0,
                                              stop=o == OB - 1 and c == 1 and i == 3)
                    mm.then_inc(pv_done[c], 1)

            turn_weights(0, lambda half: claim(prologue_fill("WQ", half)), pj_full)
            fill("XT", 0, None, prologue_fill("XT", 0), 0, None)
            turn_weights(1, lambda half: wk_ps[half], w_full)
            turn_weights(3, lambda half: wo_ps[half], w_full)
            wait_moved(pe, [prologue_fill("WQ", half) for half in range(2)])
            pe.wait_ge(w_moved, 2)
            for k in range(4):
                fill("QK", k, None, prologue_fill("QK", k), 0, None)
            scores(0, 0, 0, 0, [prologue_fill("QK", k) for k in range(4)], first=True)
            pe.wait_ge(w_loaded[2], 16)
            for h in range(2):
                for part in range(2):
                    value_weights(2 * h + part)
                for k in range(2):
                    fill("QK", 4 + 2 * h + k, None, prologue_fill("QK", 4 + 2 * h + k), 0, None)
            f = prologue_fill("RW", 0)
            bank = claim(f)
            pe.wait_ge(small_loaded, 64)
            nc.tensor.transpose(bank[:, 0:E], rw_in[:, :], ident[0:E, 0:E]).then_inc(pj_full, 1)
            wait_moved(pe, [prologue_fill("RW", 0)])
            pe.wait_ge(w_moved, 8)
            fill("V", 0, None, prologue_fill("V", 0), 0, None)
            pe.wait_ge(consts_ready, CONSTS)

            def body(bd):
                for j in range(STEPS):
                    n = bd.octet(j)
                    if not (bd.last and j == STEPS - 1):
                        m = j + 1
                        o = m % OB
                        scores(n + 1, m // OB % UB, o, m // 4, [bd.ahead("QK", k, m // 4) for k in range(4 * o, 4 * o + 4)])

                    def run(s):
                        for name, part, bb, f in bd.slot(j, s):
                            if name == "LG":
                                wait_moved(pe, [bd.find("X2T", 0, [j])])
                            if name == "RK":
                                fill(name, part, bd.unit(bb), f, bb, bd)
                            elif bb is not None:
                                fill(name, part, bd.batch(bb), f, bb, bd)
                            else:
                                fill(name, part, None, f, bd.unit_of(name, part, j), bd)

                    run("A")
                    transposes(n, j % 2, first=bd.first and j == 0)
                    run("B")
                    bb, o = divmod(j, OB)
                    values(n, bd.batch(bb), bb % UB, o, j % 2,
                           [bd.ahead("V", 4 * (bb % UB) + 2 * o + h, j // 4) for h in range(2)], early=bd.first and bb < UB)
                    run("C")

            body(FIRST)
            with pe.Fori(1, NBODY - 1) as it:
                body(Body(it))
            body(LAST)
            fill("X2T", 0, B - 1, Fill(TAIL), BB - 1, None)
            wait_moved(pe, [Fill(TAIL)])
            fill("LG", 0, B - 1, Fill(TAIL + 1), None, None)
            fill("LAST RK", 0, NUNIT - 1, Fill(TAIL + 2), None, None)
            fill("CT", 0, None, Fill(TAIL + 3), None, None)

            pe.wait_ge(gu_split, E)
            pe.wait_ge(wd_loaded, 16)
            pe.wait_ge(plan, PLAN_STEPS)
            for c in range(2):
                pe.wait_ge(exp_ready[c], NOCT)
                pe.wait_ge(probsT_ready[c], NOCT)
            pe.wait_ge(x1_ready, B)
            wait_moved(pe, [Fill(TAIL + 2), Fill(TAIL + 3)])

            def turn(t, r, arrived):
                pe.wait_ge(xt_loaded[r % RING], arrived)
                if not (isinstance(t, int) and t < 2):
                    pe.wait_ge(xt_ready, t - 1)
                nc.tensor.transpose(xt_ps[r % 2][:, 0:P], xt[:, r % RING, 0:P], ident[:, :]).then_inc(xt_turned, 1)

            wgu_flat = [w[:, :, :].rearrange("p e f -> p (e f)") for w in (wgu_hi, wgu_lo)]
            wd_flat = wd[:, :, :, :].rearrange("p e c d -> p (e c d)")

            def gate_up(t, r, e):
                pe.wait_ge(xt_ready, t + 1)
                if not (isinstance(t, int) and t < 2):
                    pe.wait_ge(hid_ready, t - 1)
                product(gu_ps[r % 2][:, :], [x[:, r % 2, :] for x in (xtT_hi, xtT_lo)],
                        [w[:, bass.ds(e * (2 * F), 2 * F)] for w in wgu_flat]).then_inc(gu_done, 1)

            def turn_hidden(t, r):
                pe.wait_ge(hid_ready, t + 1)
                if not (isinstance(t, int) and t < 2):
                    pe.wait_ge(hidT_ready, t - 1)
                for c in range(FC):
                    mm = nc.tensor.transpose(ht_ps[r % 2][:, c * P:(c + 1) * P], hid[:, r % 2, c * P:(c + 1) * P], ident[:, :])
                mm.then_inc(hid_turned, 1)

            def down(t, r, e):
                pe.wait_ge(hidT_ready, t + 1)
                if not (isinstance(t, int) and t < 2):
                    pe.wait_ge(y_ready, t - 1)
                for c in range(FC):
                    mm = nc.tensor.matmul(y_ps[r % 2][:, 0:P], hidT[:, r % 2, c * P:(c + 1) * P],
                                          wd_flat[:, bass.ds(e * (FC * P) + c * P, P)], start=c == 0, stop=c == FC - 1)
                mm.then_inc(down_done, 1)

            def tiles_body(it, first=False, last=False):
                experts = load_values(expert_of[0:1, bass.ds(it * RING, BEHIND + RING)], mybir.EngineType.PE, E - 1)
                for r in range(RING):
                    t = RING * it + r
                    if not (last and r == RING - 1):
                        turn(t + 1, r + 1, 16 * (it + (r + 1) // RING) + 16)
                    gate_up(t, r, experts[BEHIND + r])
                    if not (first and r < 1):
                        turn_hidden(t - 1, r - 1)
                    if not (first and r < 2):
                        down(t - 2, r - 2, experts[BEHIND + r - 2])
                return experts

            turn(0, 0, 16)
            tiles_body(0, first=True)
            with pe.Fori(1, NTB - 1) as it:
                tiles_body(it)
            experts = tiles_body(NTB - 1, last=True)
            turn_hidden(NT - 1, NT - 1)
            down(NT - 2, NT - 2, experts[BEHIND + RING - 2])
            down(NT - 1, NT - 1, experts[BEHIND + RING - 1])

        @block.vector
        def _(dve):
            def stats_x(u, par, arrived):
                dve.wait_ge(x_loaded[par], arrived)
                for i in range(UB):
                    op = nc.vector.bn_stats(st1[:, i, :], x_in[par][:, i, :])
                op.then_inc(stats1, 1)
                wait_apart(dve, stats1, u + 1)
                for i in range(UB):
                    nc.vector.bn_aggr(mv1[:, i, :], st1[:, i, :]).then_inc(agg1, 1)

            def norm_x(u, par):
                dve.wait_ge(rstd1, u + 1)
                for i in range(UB):
                    op = nc.vector.tensor_scalar(xn[par][:, i, :], x_in[par][:, i, :], mv1[:, i, 0:1],
                                                 rs1[:, i:i + 1], ALU.subtract, ALU.mult)
                op.then_inc(xn_ready, 1)

            def norm_x2(b, s, earlier):
                dve.wait_ge(rstd2, b + 1)
                if earlier is not None:
                    dve.wait_ge(scattered[s // UB], earlier)
                for k in range(K):
                    op = nc.vector.tensor_scalar(rows[:, s, k, 0:P], x1_all[:, bass.ds(b * P, P)], mv2[:, 0:1],
                                                 rs2[:, :], ALU.subtract, ALU.mult)
                op.then_inc(x2_ready, 1)

            def select(u, us, logits):
                for f in logits:
                    wait_apart(dve, pj_moved[f.bank], f.moved)
                for b in range(UB):
                    op = nc.vector.max(topv[:, us, b, :], lg[:, us * UB + b, :])
                op.then_inc(top_ready, 1)
                wait_apart(dve, top_ready, u + 1)
                for b in range(UB):
                    op = nc.vector.max_index(topi[:, us, b, :], topv[:, us, b, :], lg[:, us * UB + b, :])
                op.then_inc(topi_ready, 1)
                dve.wait_ge(topi_ready, u + 1)
                nc.vector.tensor_copy(topf[:, :, :], topi[:, us, :, 0:K]).then_inc(topf_ready, 1)
                dve.wait_ge(topf_ready, u + 1)
                nc.vector.tensor_tensor(chosen[:, us, :, :, :],
                                        iota_e[:, :].unsqueeze(1).unsqueeze(1).to_broadcast([P, UB, K, E]),
                                        topf[:, :, :].unsqueeze(3).to_broadcast([P, UB, K, E]), ALU.is_equal)\
                  .then_inc(chosen_ready, 1)

            def gate_unit(u, us, earlier):
                dve.wait_ge(gate_exp, u + 1)
                nc.vector.tensor_scalar(g_exp[:, us, :, :], g_exp[:, us, :, :], 1.0, None, ALU.add).then_inc(gate_chain, 1)
                dve.wait_ge(gate_chain, 4 * u + 1)
                nc.vector.reciprocal(g_sig[:, :, :], g_exp[:, us, :, :]).then_inc(gate_chain, 1)
                dve.wait_ge(gate_chain, 4 * u + 2)
                nc.vector.scalar_tensor_tensor(out=g_sum[:, :], in0=g_sig[:, :, 0], scalar=1e-10, in1=g_sig[:, :, 1],
                                               op0=ALU.add, op1=ALU.add).then_inc(gate_chain, 1)
                dve.wait_ge(gate_chain, 4 * u + 3)
                nc.vector.reciprocal(g_sum[:, :], g_sum[:, :]).then_inc(gate_chain, 1)
                dve.wait_ge(gate_chain, 4 * u + 4)
                nc.vector.scalar_tensor_tensor(out=rows[:, us * UB:(us + 1) * UB, :, GATE], in0=g_sig[:, :, :],
                                               scalar=tgates[:, 1:2],
                                               in1=g_sum[:, :].unsqueeze(2).to_broadcast([P, UB, K]),
                                               op0=ALU.mult, op1=ALU.mult).then_inc(gates_done, 1)

            def low_weights(w, half):
                at = slice(half * 512, half * 512 + 512)
                f = prologue_fill("WQ", half)
                bank, done = (pj[f.bank], pj_moved[f.bank]) if w == 0 else (wk_ps[half], w_moved)
                dve.wait_ge(w_hi_ready, 2 * w + half + 1)
                nc.vector.tensor_tensor(w_lo[w][:, at], bank[:, :], w_hi[w][:, at].bitcast(F32), ALU.subtract)\
                  .then_inc(done, 1)

            def low_values(part):
                at = slice(part * 512, part * 512 + 512)
                dve.wait_ge(w_hi_ready, 4 + part + 1)
                nc.vector.tensor_tensor(wvo_lo[:, at], vo_ps[part % 2][:, :], wvo_hi[:, at].bitcast(F32), ALU.subtract)\
                  .then_inc(w_moved, 1)

            def move(name, part, b, f, u, when=None, us=0):
                if name in ("QK", "V"):
                    if on_vector(when, part):
                        dve.wait_ge(pj_full, f.full)
                        if name == "QK" and part % 2 == 0:
                            nc.vector.tensor_scalar(projected(name, part, us), pj[f.bank][:, :], SCALE, None, ALU.mult)\
                              .then_inc(pj_moved[f.bank], 1)
                        else:
                            nc.vector.tensor_copy(projected(name, part, us), pj[f.bank][:, :]).then_inc(pj_moved[f.bank], 1)
                elif name == "XT":
                    dve.wait_ge(xcT_hi_ready, u + 1)
                    nc.vector.tensor_tensor(xcT_lo[:, :], pj[f.bank][:, :], xcT_hi[:, :].bitcast(F32), ALU.subtract)\
                      .then_inc(pj_moved[f.bank], 1)
                elif name == "LG":
                    dve.wait_ge(pj_full, f.full)
                    nc.vector.tensor_copy(lg[:, u, :], pj[f.bank][:, 0:E]).then_inc(pj_moved[f.bank], 1)
                elif name == "RK":
                    dve.wait_ge(pj_full, f.full)
                    rank = pj[f.bank][:, 0:UB * E].rearrange("p (b e) -> p b e", e=E)
                    nc.vector.tensor_tensor(ranked[:, :, :, :], rank.unsqueeze(2).to_broadcast([P, UB, K, E]),
                                            chosen[:, u, :, :, :], ALU.mult).then_inc(pj_moved[f.bank], 1)
                    dve.wait_ge(pj_moved[f.bank], f.moved)
                    with nc.allow_low_precision(reason="whole numbers below 2^24 are exact in float32"):
                        nc.vector.tensor_reduce(slot[:, u, :, :], ranked[:, :, :, :], AX.X, ALU.add).then_inc(slots_ready, 1)

            def add_attention(b, par):
                x1 = x1_all[:, bass.ds(b * P, P)]
                dve.wait_ge(pv_done[1], OB * (b + 1))
                dve.wait_ge(xb_ready, NUNIT if isinstance(b, int) and b == B - 1 else b // UB + 1)
                nc.vector.scalar_tensor_tensor(out=x1, in0=o_ps[par][:, 0:P], scalar=tgates[:, 0:1], in1=x1,
                                               op0=ALU.mult, op1=ALU.add).then_inc(x1_ready, 1)
                wait_apart(dve, x1_ready, b + 1)
                nc.vector.bn_stats(st2[:, :], x1).then_inc(stats2, 1)
                wait_apart(dve, stats2, b + 1)
                nc.vector.bn_aggr(mv2[:, :], st2[:, :]).then_inc(agg2, 1)

            def find_max(n, c):
                s = s_ps[c][:, :].rearrange("p (h k) -> p h k", h=4)
                dve.wait_ge(scored[c], n + 1)
                nc.vector.tensor_reduce(neg_max[c][:, :], s, AX.X, ALU.max, negate=True).then_inc(max_ready[c], 1)

            def normalize(n, c, par):
                p = p_buf[:, c, par, :].rearrange("p (h k) -> p h k", h=4)
                dve.wait_ge(exp_ready[c], n + 1)
                nc.vector.reciprocal(rden[c][:, :], sums[c][:, :]).then_inc(rden_ready[c], 1)
                dve.wait_ge(rden_ready[c], n + 1)
                nc.vector.tensor_tensor(p, p, rden[c][:, :].unsqueeze(2).to_broadcast([P, 4, P]), ALU.mult)\
                  .then_inc(probs_ready[c], 1)

            stats_x(0, 0, 16)
            norm_x(0, 0)
            for half in range(2):
                low_weights(0, half)
            move("XT", 0, None, prologue_fill("XT", 0), 0)
            for half in range(2):
                low_weights(1, half)
            for half in range(2):
                dve.wait_ge(w_full, 2 + half + 1)
                nc.vector.tensor_copy(woT[:, 4 * half:4 * half + 4, :].rearrange("p c d -> p (c d)"), wo_ps[half][:, :])\
                  .then_inc(w_moved, 1)
            for k in range(4):
                move("QK", k, None, prologue_fill("QK", k), 0)
            stats_x(1, 1, 16)
            for c in range(2):
                find_max(0, c)
            dve.wait_ge(small_loaded, 64)
            dve.wait_ge(gates_ready, 1)
            nc.vector.tensor_scalar(bo_t[:, :], bo_b[:, :], tgates[:, 0:1], None, ALU.mult).then_inc(bias_ready, 1)
            for c in range(2):
                low_values(2 * c)
                low_values(2 * c + 1)
                for k in range(2):
                    move("QK", 4 + 2 * c + k, None, prologue_fill("QK", 4 + 2 * c + k), 0)
                normalize(0, c, 0)
            f = prologue_fill("RW", 0)
            dve.wait_ge(pj_full, f.full)
            nc.vector.tensor_copy(rwT[:, :], pj[f.bank][:, 0:E]).then_inc(pj_moved[f.bank], 1)
            norm_x(1, 1)

            def body(bd):
                for j in range(STEPS):
                    n = bd.octet(j)
                    more = not (bd.last and j == STEPS - 1)
                    bb = j // OB - 1
                    if more:
                        for c in range(2):
                            find_max(n + 1, c)

                    def run(s):
                        for name, part, bb, f in bd.slot(j, s):
                            if name == "RK":
                                move(name, part, bd.unit(bb), f, bb % BU)
                            elif name == "LG":
                                move(name, part, bd.batch(bb), f, bb % BB)
                            else:
                                b = None if bb is None else bd.batch(bb)
                                move(name, part, b, f, bd.unit(j // 4 + 1), s, bd.unit_of(name, part, j))

                    run("A")
                    if j % 4 == 2 and not (bd.first and j < 4):
                        select(bd.unit(j // 4 - 1), (j // 4 + 1) % BU, [bd.find("LG", 0, [j - k]) for k in (3, 1)])
                    run("B")
                    if more:
                        for c in range(2):
                            normalize(n + 1, c, (j + 1) % 2)
                    if j % OB == 1:
                        add_attention(bd.batch(j // OB), j // OB % 2)
                    run("C")
                    if j % 4 == 3 and not (bd.first and j < 4):
                        gate_unit(bd.unit(j // 4 - 1), (j // 4 + 1) % BU, None)
                    if j % OB == 0 and not (bd.first and bb < 0):
                        norm_x2(bd.batch(bb), bb % BB, None if bd.first or (bd.second and bb < 0) else
                                16 * UB * K * (bd.it + (-1 if bb < 0 else 0)))
                    if j % 4 == 1 and not bd.last:
                        norm_x(bd.unit(j // 4 + 2), j // 4)
                    if j % 4 == 0 and not bd.last:
                        us = j // 4
                        stats_x(bd.unit(us + 2), us, 16 * bd.it + 32)

            body(FIRST)
            body(SECOND)
            with dve.Fori(2, NBODY - 1) as it:
                body(Body(it))
            body(LAST)
            norm_x2(B - 1, BB - 1, 16 * UB * K * (NBODY - 1))
            move("LG", 0, B - 1, Fill(TAIL + 1), BB - 1)
            select(NUNIT - 1, BU - 1, [LAST.find("LG", 0, [STEPS - 1]), Fill(TAIL + 1)])
            dve.wait_ge(slots_ready, NUNIT - 1)
            dve.wait_ge(chosen_ready, NUNIT)
            nc.vector.tensor_tensor(count[:, :, :], chosen[:, BU - 1, :, 0, :], chosen[:, BU - 1, :, 1, :], ALU.add)\
              .then_inc(last_count, 1)
            gate_unit(NUNIT - 1, BU - 1, None)
            move("RK", 0, NUNIT - 1, Fill(TAIL + 2), BU - 1)

            steps = [0]

            def step(op):
                op.then_inc(plan, 1)
                steps[0] += 1
                dve.wait_ge(plan, steps[0])

            f = Fill(TAIL + 3)
            dve.wait_ge(pj_full, f.full)
            step(nc.vector.tensor_copy(pads_at[:, :], pj[f.bank][:, 0:E]))
            nc.vector.tensor_tensor(ends[:, :], pj[f.bank][:, 0:E], region_at[:, :], ALU.subtract)\
              .then_inc(pj_moved[f.bank], 1)
            dve.wait_ge(pj_moved[f.bank], f.moved)
            step(nc.vector.tensor_tensor(tiles_tmp[:, :, :], ends[:, :].unsqueeze(2).to_broadcast([P, E, NOF]),
                                         thresholds[:, :, :], ALU.is_gt))
            step(nc.vector.tensor_reduce(tiles[:, :], tiles_tmp[:, :, :], AX.X, ALU.add))
            step(nc.vector.tensor_tensor(tiles_tmp2[:, :, :], tiles[:, :].unsqueeze(1).to_broadcast([P, E, E]),
                                         upto[:, :, :], ALU.mult))
            step(nc.vector.tensor_reduce(tiles_upto[:, :], tiles_tmp2[:, :, :], AX.X, ALU.add))
            step(nc.vector.tensor_tensor(past[:, :, :], tiles_upto[:, :].unsqueeze(1).to_broadcast([P, NT, E]),
                                         iota_t[:, :, :], ALU.is_le))
            step(nc.vector.tensor_reduce(tile_e[:, :], past[:, :, :], AX.X, ALU.add))
            step(nc.vector.tensor_scalar(expert_of[:, BEHIND:BEHIND + NT], tile_e[:, :], float(E - 1), None, ALU.min))
            step(nc.vector.tensor_tensor(past[:, :, :], past[:, :, :], tiles[:, :].unsqueeze(1).to_broadcast([P, NT, E]),
                                         ALU.mult))
            step(nc.vector.tensor_reduce(tile_before[:, :], past[:, :, :], AX.X, ALU.add))
            step(nc.vector.scalar_tensor_tensor(out=tile_e[:, :], in0=tile_e[:, :], scalar=float(REGION), in1=row_t[:, :],
                                                op0=ALU.mult, op1=ALU.add))
            step(nc.vector.scalar_tensor_tensor(out=first_row[:, :], in0=tile_before[:, :], scalar=-float(P),
                                                in1=tile_e[:, :], op0=ALU.mult, op1=ALU.add))
            assert steps[0] == PLAN_STEPS

            def low(t, r):
                dve.wait_ge(xt_hi_ready, t + 1)
                nc.vector.tensor_tensor(xtT_lo[:, r % 2, :], xt_ps[r % 2][:, 0:P], xtT_hi[:, r % 2, :].bitcast(F32),
                                        ALU.subtract).then_inc(xt_ready, 1)

            def hidden(t, r):
                dve.wait_ge(silu_ready, t + 1)
                if not (isinstance(t, int) and t < 2):
                    dve.wait_ge(hid_turned, t - 1)
                nc.vector.tensor_tensor(hid[:, r % 2, :], silu[:, r % 2, :], gu_ps[r % 2][:, F:2 * F], ALU.mult)\
                  .then_inc(hid_ready, 1)

            def gated(t, r, earlier):
                dve.wait_ge(down_done, t + 1)
                if earlier is not None:
                    dve.wait_ge(y_scattered[r % RING], earlier)
                nc.vector.tensor_scalar(y[:, r % RING, :], y_ps[r % 2][:, 0:P], xt[:, r % RING, GATE:GATE + 1], None,
                                        ALU.mult).then_inc(y_ready, 1)

            def tiles_body(it, first=False, last=False, second=False):
                for r in range(RING):
                    t = RING * it + r
                    if not (last and r == RING - 1):
                        low(t + 1, r + 1)
                    hidden(t, r)
                    if not (first and r < 2):
                        early = first or (second and r < 2)
                        gated(t - 2, r - 2, None if early else 16 * (it + (-1 if r < 2 else 0)))

            low(0, 0)
            tiles_body(0, first=True)
            tiles_body(1, second=True)
            with dve.Fori(2, NTB - 1) as it:
                tiles_body(it)
            tiles_body(NTB - 1, last=True)
            gated(NT - 2, NT - 2, 16 * (NTB - 1))
            gated(NT - 1, NT - 1, 16 * (NTB - 1))

            for g in range(NG):
                both = y12[:, g, :, :]
                dve.wait_ge(y12_loaded[g], 16 * K)
                nc.vector.tensor_tensor(both[:, 0, :], x1_all[:, g * GT * P:(g + 1) * GT * P], both[:, 0, :], ALU.add)\
                  .then_inc(part_ready, 1)
                dve.wait_ge(part_ready, g + 1)
                nc.vector.tensor_tensor(both[:, 1, :], both[:, 0, :], both[:, 1, :], ALU.add).then_inc(total_ready, 1)


_INS = ["x", "ctx_1024", "g_xattn", "g_ffn", "L0_xattn_Wq", "L0_xattn_Wk", "L0_xattn_Wv", "L0_xattn_Wo", "L0_xattn_bo",
        "L0_ffn_router_w", "L0_ffn_w_gate", "L0_ffn_w_up", "L0_ffn_w_down"]


def kernel(**inputs):
    import numpy as _np
    import concourse.bacc as _bacc
    from concourse import mybir as _mybir
    from concourse.bass_utils import run_bass_kernel_spmd as _run

    nc = _bacc.Bacc("TRN2", target_bir_lowering=False, num_devices=1)
    arrays, args = {}, []
    for name in _INS:
        a = _np.ascontiguousarray(inputs[name])
        arrays[f"in_{name}"] = a
        args.append(nc.dram_tensor(f"in_{name}", a.shape, _mybir.dt.from_np(a.dtype), kind="ExternalInput").ap())
    args.append(nc.dram_tensor("out_0", (B, P, P), F32, kind="ExternalOutput").ap())
    args.append(nc.dram_tensor("sorted_rows", (E * REGION + SPARE * P, ROW), F32, kind="Internal").ap())
    args.append(nc.dram_tensor("results", (NOWHERE + (E + SPARE) * P, P), F32, kind="Internal").ap())
    build(nc, *args)
    r = _run(nc, [arrays], core_ids=[0])
    return r.results[0]["out_0"]
```

```python
from contextlib import ExitStack

import concourse.bass as bass
from concourse import mybir

F32 = mybir.dt.float32
F32R = mybir.dt.float32r
U32 = mybir.dt.uint32
I32 = mybir.dt.int32
ALU = mybir.AluOpType
ACT = mybir.ActivationFunctionType
AX = mybir.AxisListType

P = 128
B = 32
H, HD = 16, 64
NCH = H * HD // P
E, F = 8, 256
FC = F // P
EPS = 1e-5
ROOT_STEPS = 5
SCALE = 1.0 / HD ** 0.5

UB = 2
BU = 2
BB = UB * BU
OB = 2
STEPS = BB * OB
NBODY = B // BB
NOCT = B * OB
NUNIT = B // UB

K = 2
TOKENS = B * P
LATE = 2
UNITS = [NUNIT - LATE, LATE]
REGION = [u * UB * P + P for u in UNITS]
NOF = [u * UB for u in UNITS]
NT = [u * UB * K + E for u in UNITS]
T = sum(NT)
RING = 8
BEHIND = 2
NTB = [t // RING for t in NT]
TB = sum(NTB)
SPARE = E
DEST, GATE, ROW = P, P + 1, P + 2
NOWHERE = K * TOKENS
assert all(t % RING == 0 for t in NT) and RING == E

GT = 4
NG = B // GT
DONE = UNITS[0] * UB // GT
SOON = 2
BESIDE = 3
assert UNITS[0] * UB % GT == 0 and max(SOON, BESIDE) < RING
PLAN_STEPS = 13
CONSTS = 19
LATE_AT = 5


def fills_at(j, first, last):
    q, bb, even = j % (UB * OB), j // OB, j % OB == 0
    slots = {"A": [], "B": [], "C": []}
    if not even and not (first and bb < 1):
        slots["A"].append(("X2T", 0, bb - 1))
    if not even and not (first and bb < 1):
        slots["B"].append(("LG", 0, bb - 1))
    due = {
        0: {"A": [("V", 1)], "B": [("V", 2), ("V", 3)], "C": [("V", 4), ("V", 5)]},
        1: {"A": [("V", 6)], "B": [("V", 7)]},
        2: {}, 3: {},
    }[q]
    ahead = {
        0: {},
        1: {"B": [("XT", 0)], "C": [("QK", 0)]},
        2: {"A": [("QK", 1)], "B": [("QK", 2), ("QK", 3)], "C": [("QK", 4)]},
        3: {"A": [("QK", 5)], "B": [("QK", 6), ("QK", 7)], "C": [("V", 0)]},
    }[q]
    for s, parts in due.items():
        slots[s] += [(name, part, None) for name, part in parts]
    if q == 3 and not (first and j < 4):
        slots["C"].append(("RK", 0, j // 4 - 1))
    if last and j == UB * OB:
        slots["B"].append(("CT", 0, 0))
    if not (last and j >= UB * OB):
        for s, parts in ahead.items():
            slots[s] += [(name, part, None) for name, part in parts]
    return slots


def fills_of(first, last):
    return [(j, s, n) for j in range(STEPS) for s, parts in fills_at(j, first, last).items() for n, _ in enumerate(parts)]


PROLOGUE = [(name, part) for name, parts in
            [("WQ", 2), ("XT", 1), ("QK", 8), ("RW", 1), ("V", 1)] for part in range(parts)]
AHEAD = len(PROLOGUE)
N_FIRST = len(fills_of(True, False))
N_MID = len(fills_of(False, False))
N_LAST = len(fills_of(False, True))
assert N_MID % 2 == 0
BASE = AHEAD + N_FIRST - N_MID
TAIL = BASE + N_MID * (NBODY - 1) + N_LAST


class Fill:

    def __init__(self, fixed, it=0):
        self.bank = fixed % 2
        self.full = N_MID * it + (fixed + 1)
        self.moved = (N_MID // 2) * it + (fixed // 2 + 1)
        self.before = None if isinstance(it, int) and it == 0 and fixed < 2 else (N_MID // 2) * it + fixed // 2
        self.order = fixed


class LateFill:

    def __init__(self, k):
        self.bank, self.full, self.moved, self.before, self.order = 2, TAIL + k + 1, k + 1, k or None, k


class Body:

    def __init__(self, it, first=False, last=False, second=False):
        self.it, self.first, self.last, self.second = it, first, last, second
        self.plan = fills_of(first, last)

    def slot(self, j, s):
        return [(name, part, bb, self.fill(self.plan.index((j, s, n))))
                for n, (name, part, bb) in enumerate(fills_at(j, self.first, self.last)[s])]

    def fill(self, at):
        return Fill(AHEAD + at) if self.first else Fill(BASE + at, self.it)

    def find(self, name, part, steps):
        for j in steps:
            kind = (False, False) if j < 0 else (self.first, self.last)
            for s, parts in fills_at(j % STEPS, *kind).items():
                for n, entry in enumerate(parts):
                    if entry[:2] == (name, part):
                        at = fills_of(*kind).index((j % STEPS, s, n))
                        return Fill(BASE - N_MID + at, self.it) if j < 0 else self.fill(at)

    def ahead(self, name, part, us):
        if us == 0 and self.first and not (name == "V" and part > 0):
            return prologue_fill(name, part)
        late = name == "V" and part > 0
        return self.find(name, part, range(4 * us, 4 * us + 2) if late else range(4 * us - 3, 4 * us))

    def octet(self, j):
        return STEPS * self.it + j

    def batch(self, bb):
        return BB * self.it + bb

    def unit(self, us):
        return BU * self.it + us

    def unit_of(self, name, part, j):
        return j // 4 if name == "V" and part > 0 else j // 4 + 1


def on_vector(when, part):
    return part % 2 == 1 if when is None else when in "AB"


def prologue_fill(name, part):
    return Fill(PROLOGUE.index((name, part)))


def build(nc, x, ctxt, g_xattn, g_ffn, Wq, Wk, Wv, Wo, bo, router_w, w_gate, w_up, w_down, out, sorted_rows, results):
    with ExitStack() as ctx:
        def sb(name, shape, dt=F32):
            return ctx.enter_context(nc.sbuf_tensor(name, shape, dt))

        def ps(name):
            return ctx.enter_context(nc.psum_tensor(name, [P, 512], F32))

        def sem(name):
            return ctx.enter_context(nc.semaphore(name))

        ident = sb("ident", [P, P])
        gates = sb("gates", [P, 2])
        tgates = sb("tgates", [P, 2])
        bo_b = sb("bo_b", [P, P])
        bo_t = sb("bo_t", [P, P])
        rw_in = sb("rw_in", [E, P])
        rwT = sb("rwT", [P, E])
        w_hi = [sb(f"w{c}_hi", [P, NCH * P], F32R) for c in "qk"]
        w_lo = [sb(f"w{c}_lo", [P, NCH * P], F32R) for c in "qk"]
        wvo_hi = sb("wvo_hi", [P, H * P], F32R)
        wvo_lo = sb("wvo_lo", [P, H * P], F32R)
        wgu_hi = sb("wgu_hi", [P, E, 2 * F], F32R)
        wgu_lo = sb("wgu_lo", [P, E, 2 * F], F32R)
        wd = sb("wd", [P, E, FC, P])
        x1_all = sb("x1_all", [P, B * P])
        gu_places = x1_all[:, :].rearrange("p (e f) -> p e f", e=E)
        gu_stage = [gu_places[:, 1 + (e if e < E - 1 else 1), :] for e in range(E)]
        x_in = [sb(f"x_in{i}", [P, UB, P]) for i in range(2)]
        c_in = [sb(f"c_in{i}", [P, UB, P]) for i in range(2)]
        xn = [sb(f"xn{i}", [P, UB, P]) for i in range(2)]
        st1 = sb("st1", [P, UB, 6])
        mv1 = sb("mv1", [P, UB, 2])
        ve1, rs1, nt1 = (sb(s, [P, UB]) for s in ("ve1", "rs1", "nt1"))
        xcT_hi = sb("xcT_hi", [P, 2 * UB * P], F32R)
        xcT_lo = sb("xcT_lo", [P, 2 * UB * P], F32R)
        qkT = sb("qkT", [P, 2, 2, NCH, UB * P])
        v = sb("v", [P, UB, H, P])
        woT = v[:, 1, 0:8, :]
        neg_max = [sb(f"neg_max{c}", [P, 4]) for c in "ab"]
        sums = [sb(f"sums{c}", [P, 4]) for c in "ab"]
        p_buf = sb("p_buf", [P, 2, 2, 512])
        pT_buf = sb("pT_buf", [P, 2, 2, 512])
        w_stage = [(p_buf, pT_buf)[w // 2][:, w % 2, :, :].rearrange("p a b -> p (a b)")
                   .rearrange("p (c d) -> p c d", c=NCH) for w in range(4)]
        rden = [sb(f"rden{c}", [P, 4]) for c in "ab"]
        st2 = sb("st2", [P, 6])
        mv2 = sb("mv2", [P, 2])
        minus_half = sb("minus_half", [P, UB])
        ve2, rs2, nt2 = (sb(s, [P, 1]) for s in ("ve2", "rs2", "nt2"))
        rows = sb("rows", [P, BB, K, ROW])
        x2T = sb("x2T", [P, P])
        iota_e = sb("iota_e", [P, E])
        before = sb("before", [P, P])
        ones = sb("ones", [P, P])
        dest = sb("dest", [P, B, K], U32)
        lg = sb("lg", [P, BB, E])
        topv = sb("topv", [P, BU, UB, 8])
        topi = sb("topi", [P, BU, UB, 8], U32)
        topf = sb("topf", [P, UB, K])
        chosen = sb("chosen", [P, BU, UB, K, E])
        count = sb("count", [P, UB, E])
        counted = sb("counted", [P, UB + 1, E])
        ranked = sb("ranked", [P, UB, K, E])
        slot = sb("slot", [P, BU, UB, K], U32)
        g_exp = sb("g_exp", [P, BU, UB, K])
        g_sig = sb("g_sig", [P, UB, K])
        g_sum = sb("g_sum", [P, UB])
        region_at = sb("region_at", [P, len(UNITS), E])
        late_start = sb("late_start", [P, E])
        thresholds = sb("thresholds", [P, E, NOF[0]])
        upto = sb("upto", [P, E, E])
        iota_t = sb("iota_t", [P, NT[0], E])
        row_t = sb("row_t", [P, NT[0]])
        row_ends = sb("row_ends", [P, E])
        ends = sb("ends", [P, E])
        pads_at = sb("pads_at", [P, len(UNITS), E], I32)
        tiles_tmp = sb("tiles_tmp", [P, E, NOF[0]])
        tiles = sb("tiles", [P, E])
        tiles_tmp2 = sb("tiles_tmp2", [P, E, E])
        tiles_upto = sb("tiles_upto", [P, E])
        past = sb("past", [P, NT[0], E])
        tile_e = sb("tile_e", [P, NT[0]])
        tile_before = sb("tile_before", [P, NT[0]])
        expert_of = sb("expert_of", [P, BEHIND + T], I32)
        first_row = sb("first_row", [P, T], I32)
        pad_rows = sb("pad_rows", [P, E + SPARE, ROW])
        xt = sb("xt", [P, RING, ROW])
        xtT_hi = sb("xtT_hi", [P, 2, P], F32R)
        xtT_lo = sb("xtT_lo", [P, 2, P], F32R)
        silu = sb("silu", [P, 2, F])
        scrap = sb("scrap", [P, 1])
        hid = sb("hid", [P, 2, F])
        hidT = sb("hidT", [P, 2, F])
        y = sb("y", [P, RING, P])
        places = sb("places", [P, RING], U32)
        y12 = qkT[:, :, :, :, :].rearrange("p i w c t -> p (i w c t)")\
            .rearrange("p (g k d) -> p g k d", g=NG, k=K)

        s_ps = [ps("sa"), ps("sb")]
        t_ps = [ps("ta"), ps("tb")]
        o_ps = [ps("oa"), ps("ob")]
        pj = [ps("pj0"), ps("pj1")]
        wk_ps, wo_ps, vo_ps = s_ps, t_ps, o_ps
        gu_ps, xt_ps, ht_ps, y_ps = s_ps, t_ps[0], o_ps, pj
        fill_ps = pj + [t_ps[1]]

        w_loaded = [sem(f"w{c}_loaded") for c in "qkvo"]
        small_loaded = sem("small_loaded")
        gates_ready = sem("gates_ready")
        bias_ready = sem("bias_ready")
        ident_ready = sem("ident_ready")
        consts_ready = sem("consts_ready")
        gu_loaded = [sem(f"gu_loaded{e}") for e in range(E)]
        gu_split = sem("gu_split")
        gu_hi_done = sem("gu_hi_done")
        wd_loaded = sem("wd_loaded")
        x_loaded = [sem(f"x_loaded{i}") for i in range(2)]
        c_loaded = [sem(f"c_loaded{i}") for i in range(2)]
        stats1, agg1, rstd1, xn_ready = (sem(s) for s in ("stats1", "agg1", "rstd1", "xn_ready"))
        root1, root2 = sem("root1"), sem("root2")
        xb_ready = sem("xb_ready")
        ctxT_taken = sem("ctxT_taken")
        pj_full = sem("pj_full")
        pj_moved = [sem(f"pj_moved{i}") for i in range(3)]
        w_hi_ready = sem("w_hi_ready")
        w_full, w_moved = sem("w_full"), sem("w_moved")
        xcT_hi_ready = sem("xcT_hi_ready")
        scored = [sem(f"scored{c}") for c in "ab"]
        max_ready = [sem(f"max_ready{c}") for c in "ab"]
        exp_ready = [sem(f"exp_ready{c}") for c in "ab"]
        probs_ready = [sem(f"probs_ready{c}") for c in "ab"]
        transposed = [sem(f"transposed{c}") for c in "ab"]
        probsT_ready = [sem(f"probsT_ready{c}") for c in "ab"]
        pv_done = [sem(f"pv_done{c}") for c in "ab"]
        rden_ready = [sem(f"rden_ready{c}") for c in "ab"]
        x1_ready, stats2, agg2, rstd2, x2_ready = (sem(s) for s in ("x1_ready", "stats2", "agg2", "rstd2", "x2_ready"))
        top_ready, topi_ready, topf_ready, chosen_ready = (
            sem(n) for n in ("top_ready", "topi_ready", "topf_ready", "chosen_ready"))
        count_chain, counted_ready = sem("count_chain"), sem("counted_ready")
        last_count, late_ends = sem("last_count"), sem("late_ends")
        slots_ready = sem("slots_ready")
        gate_exp, gate_chain, gates_done = sem("gate_exp"), sem("gate_chain"), sem("gates_done")
        dest_ready = sem("dest_ready")
        scattered = [sem(f"scattered{i}") for i in range(BU)]
        spare_written = sem("spare_written")
        pads_written = sem("pads_written")
        plan = sem("plan")
        xt_loaded = [sem(f"xt_loaded{i}") for i in range(RING)]
        xt_turned, xt_hi_ready, xt_ready = sem("xt_turned"), sem("xt_hi_ready"), sem("xt_ready")
        table_in = sem("table_in")
        gu_done, silu_ready, hid_ready = sem("gu_done"), sem("silu_ready"), sem("hid_ready")
        hid_turned, hidT_ready, down_done = sem("hid_turned"), sem("hidT_ready"), sem("down_done")
        y_ready = sem("y_ready")
        y_scattered = [sem(f"y_scattered{i}") for i in range(RING)]
        y12_loaded = [sem(f"y12_loaded{i}") for i in range(NG)]
        part_ready, total_ready = sem("part_ready"), sem("total_ready")
        out_stored = sem("out_stored")
        passed = sem("passed")

        block = ctx.enter_context(nc.Block())

        def load_values(table, engine, most):
            return nc.values_load_multi_w_load_instructions(
                table, engines=[engine], min_val=0, max_val=most,
                skip_runtime_bounds_check_because="the tables' entries are clamped where they are made")[1]

        def projected(name, part, us):
            if name == "QK":
                return qkT[:, us % 2, part % 2, part // 2 * 2:part // 2 * 2 + 2, :].rearrange("p c t -> p (c t)")
            return v[:, part // 4, part % 4 * 4:part % 4 * 4 + 4, :].rearrange("p h d -> p (h d)")

        def wait_moved(eng, fills):
            for bank in range(3):
                of = [f for f in fills if f.bank == bank]
                if of:
                    eng.wait_ge(pj_moved[bank], max(of, key=lambda f: f.order).moved)

        def wait_apart(eng, waited, value):
            eng.wait_ge(waited, value)
            eng.sem_inc(passed, 1)

        FIRST, SECOND, LAST = Body(0, first=True), Body(1, second=True), Body(NBODY - 1, last=True)

        @block.sync
        def _(sp):
            def load(u, par):
                sp.dma_start(x_in[par][:, :, :], x[bass.ds(u * UB, UB)].rearrange("b t d -> t b d"))\
                  .then_inc(x_loaded[par], 16)
                sp.dma_start(c_in[par][:, :, :], ctxt[bass.ds(u * UB, UB)].rearrange("b t d -> t b d"))\
                  .then_inc(c_loaded[par], 16)

            load(0, 0)
            sp.dma_start(w_stage[0], Wq.rearrange("(c p) d -> p c d", p=P)).then_inc(w_loaded[0], 16)
            sp.dma_start(w_stage[1], Wk.rearrange("(c p) d -> p c d", p=P)).then_inc(w_loaded[1], 16)
            sp.dma_start(w_stage[3], Wo.rearrange("p (c d) -> p c d", d=P)).then_inc(w_loaded[3], 16)
            sp.dma_start(w_stage[2], Wv.rearrange("(c p) d -> p c d", p=P)).then_inc(w_loaded[2], 16)
            load(1, 1)
            for e in range(E):
                if e == E - 1:
                    sp.dma_start(wd[:, :, :, :], w_down.rearrange("e (c p) d -> p e c d", p=P)).then_inc(wd_loaded, 16)
                    sp.wait_ge(gu_split, 2)
                sp.dma_start(gu_stage[e][:, 0:F], w_gate[e]).then_inc(gu_loaded[e], 16)
                sp.dma_start(gu_stage[e][:, F:2 * F], w_up[e]).then_inc(gu_loaded[e], 16)
            with sp.Fori(1, NUNIT // 2) as i:
                for par in range(2):
                    sp.wait_ge(xn_ready, 2 * i + (par - 1))
                    sp.wait_ge(xb_ready, 2 * i + (par - 1))
                    sp.wait_ge(ctxT_taken, 2 * i + (par - 1))
                    load(2 * i + par, par)

            def write_spares(n):
                sp.dma_start(sorted_rows[n][E * REGION[n]:E * REGION[n] + SPARE * P].rearrange("(n p) w -> p n w", p=P),
                             pad_rows[:, E:E + SPARE, :]).then_inc(spare_written, 16)

            def find_pads(n):
                sp.wait_ge(plan, PLAN_STEPS * n + 1)
                return load_values(pads_at[0:1, n, :], mybir.EngineType.SP, E * REGION[n])

            def write_pads(n, e, at):
                sp.dma_start(sorted_rows[n][bass.ds(at[e], P), :], pad_rows[:, e, :]).then_inc(pads_written, 16)

            def wait_sorted(n):
                sp.wait_ge(plan, PLAN_STEPS * (n + 1))
                for us in range(BU):
                    sp.wait_ge(scattered[us], 16 * UB * K * sum(UNITS[:n + 1]) // BU)
                sp.wait_ge(pads_written, 16 * E * (n + 1))
                sp.wait_ge(spare_written, 16 * (n + 1))

            def load_tiles(n, it, first=False, beside=None):
                starts = load_values(first_row[0:1, bass.ds(it * RING, RING)], mybir.EngineType.SP,
                                     E * REGION[n] + (SPARE - 1) * P)
                for r in range(RING):
                    if not first:
                        sp.wait_ge(y_ready, RING * (it - 1) + (r + 1))
                    sp.dma_start(xt[:, r, :], sorted_rows[n][bass.ds(starts[r], P), :]).then_inc(xt_loaded[r], 16)
                    if beside:
                        beside(r)

            sp.wait_ge(consts_ready, CONSTS)
            write_spares(0)
            at = find_pads(0)
            for e in range(E):
                write_pads(0, e, at)
            wait_sorted(0)
            load_tiles(0, 0, first=True)
            with sp.Fori(1, LATE_AT + 1) as it:
                load_tiles(0, it)
            sp.wait_ge(consts_ready, CONSTS + 1)
            write_spares(1)
            at = find_pads(1)
            load_tiles(0, LATE_AT + 1, beside=lambda r: write_pads(1, r, at))
            with sp.Fori(LATE_AT + 2, NTB[0]) as it:
                load_tiles(0, it)
            wait_sorted(1)
            with sp.Fori(NTB[0], TB - 1) as it:
                load_tiles(1, it)

            both = results[0:K * TOKENS].rearrange("(k b t) d -> t k b d", k=K, t=P)

            def load_results(g):
                for k in range(K):
                    sp.dma_start(y12[:, g, k, :].rearrange("p (b d) -> p b d", d=P),
                                 both[:, k, g * GT:(g + 1) * GT, :]).then_inc(y12_loaded[g], 16)

            for r in range(RING):
                sp.wait_ge(y_scattered[r], 16 * NTB[0])
            load_tiles(1, TB - 1, beside=lambda r: load_results(r) if r < BESIDE else None)
            for g in range(BESIDE, DONE):
                load_results(g)
            for r in range(RING):
                sp.wait_ge(y_scattered[r], 16 * TB)
            for g in range(DONE, NG):
                load_results(g)

        @block.gpsimd
        def _(pool):
            nc.gpsimd.memset(ident[:, :], 0.0).then_inc(consts_ready, 1)
            pool.wait_ge(consts_ready, 1)
            nc.gpsimd.affine_select(out=ident[:, :], in_=ident[:, :], compare_op=ALU.not_equal, fill=1.0,
                                    base=0, pattern=[[-1, P]], channel_multiplier=1).then_inc(ident_ready, 1)
            nc.gpsimd.memset(minus_half[:, :], -0.5).then_inc(consts_ready, 1)

            def inverse_root(k, n, counted, agg, chain, done, var, ve, rs, nt):
                at = [0]

                def step(op, last=False):
                    if last:
                        return op.then_inc(done, 1)
                    op.then_inc(chain, 1)
                    at[0] += 1
                    wait_apart(pool, chain, ROOT_STEPS * k + at[0])

                wait_apart(pool, agg, counted)
                step(nc.gpsimd.tensor_scalar(ve, var, EPS, None, ALU.add))
                step(nc.gpsimd.tensor_tensor(rs, ve, minus_half[:, 0:n], ALU.pow))
                step(nc.gpsimd.tensor_tensor(nt, ve, rs, ALU.mult))
                step(nc.gpsimd.tensor_tensor(nt, nt, rs, ALU.mult))
                step(nc.gpsimd.tensor_scalar(nt, nt, -0.5, 1.5, ALU.mult, ALU.add))
                step(nc.gpsimd.tensor_tensor(rs, rs, nt, ALU.mult), last=True)

            def root_x(u):
                inverse_root(u, UB, UB * (u + 1), agg1, root1, rstd1, mv1[:, :, 1], ve1[:, :], rs1[:, :], nt1[:, :])

            def root_x2(b):
                inverse_root(b, 1, b + 1, agg2, root2, rstd2, mv2[:, 1:2], ve2[:, :], rs2[:, :], nt2[:, :])

            pool.wait_ge(consts_ready, 2)
            root_x(0)
            nc.gpsimd.memset(ones[:, :], 1.0).then_inc(consts_ready, 1)
            nc.gpsimd.memset(before[:, :], 1.0).then_inc(consts_ready, 1)
            nc.gpsimd.memset(upto[:, :, :], 1.0).then_inc(consts_ready, 1)
            nc.gpsimd.memset(pad_rows[:, :, :], 0.0).then_inc(consts_ready, 1)
            nc.gpsimd.memset(expert_of[:, 0:BEHIND], 0).then_inc(consts_ready, 1)

            def iota(t, pattern, channel=0):
                nc.gpsimd.iota(t, pattern, base=0, channel_multiplier=channel,
                               allow_small_or_imprecise_dtypes=True).then_inc(consts_ready, 1)

            iota(iota_e[:, :], [[1, E]])
            iota(dest[:, :, :], [[P, B], [TOKENS, K]], 1)
            for n in range(len(UNITS)):
                iota(region_at[:, n, :], [[REGION[n], E]])
            iota(thresholds[:, :, :], [[0, E], [P, NOF[0]]])
            iota(iota_t[:, :, :], [[1, NT[0]], [0, E]])
            iota(row_t[:, :], [[P, NT[0]]])
            iota(counted[:, UB, :], [[REGION[0] // P, E]])
            iota(late_start[:, :], [[REGION[1] // P, E]])
            pool.wait_ge(consts_ready, CONSTS - 3)
            nc.gpsimd.affine_select(out=before[:, :], in_=before[:, :], compare_op=ALU.is_gt, fill=0.0,
                                    base=0, pattern=[[1, P]], channel_multiplier=-1).then_inc(consts_ready, 1)
            nc.gpsimd.affine_select(out=upto[:, :, :], in_=upto[:, :, :], compare_op=ALU.is_ge, fill=0.0,
                                    base=0, pattern=[[1, E], [-1, E]], channel_multiplier=0).then_inc(consts_ready, 1)

            def pad_places(n):
                nc.gpsimd.iota(pad_rows[:, :, DEST].bitcast(U32), [[P, E + SPARE]],
                               base=NOWHERE + n * (E + SPARE) * P, channel_multiplier=1).then_inc(consts_ready, 1)

            pad_places(0)

            def residual(u, par, arrived):
                pool.wait_ge(x_loaded[par], arrived)
                nc.gpsimd.tensor_tensor(x1_all[:, bass.ds(u * (UB * P), UB * P)].rearrange("p (b d) -> p b d", b=UB),
                                        x_in[par][:, :, :], bo_t[:, :].unsqueeze(1).to_broadcast([P, UB, P]),
                                        ALU.add).then_inc(xb_ready, 1)

            def count_unit(u, us):
                pool.wait_ge(chosen_ready, u + 1)
                if not (isinstance(u, int) and u == 0):
                    pool.wait_ge(slots_ready, u)
                nc.gpsimd.tensor_tensor(count[:, :, :], chosen[:, us, :, 0, :], chosen[:, us, :, 1, :], ALU.add)\
                  .then_inc(count_chain, 1)
                late = isinstance(u, int) and u == UNITS[0]
                if late:
                    pool.wait_ge(plan, 1)
                nc.gpsimd.tensor_copy(counted[:, 0, :], late_start[:, :] if late else counted[:, UB, :])\
                  .then_inc(count_chain, 1)
                for b in range(UB):
                    pool.wait_ge(count_chain, (UB + 1) * u + (2 + b))
                    nc.gpsimd.tensor_tensor(counted[:, b + 1, :], counted[:, b, :], count[:, b, :], ALU.add)\
                      .then_inc(count_chain if b < UB - 1 else counted_ready, 1)

            def scatter_unit(u, us, earlier, n=0):
                if earlier is not None:
                    wait_apart(pool, scattered[us], earlier)
                nc.gpsimd.tensor_copy(rows[:, us * UB:(us + 1) * UB, :, DEST].bitcast(U32),
                                      dest[:, bass.ds(u * UB, UB), :]).then_inc(dest_ready, 1)
                pool.wait_ge(dest_ready, u + 1)
                pool.wait_ge(gates_done, u + 1)
                pool.wait_ge(x2_ready, UB * (u + 1))
                wait_apart(pool, slots_ready, u + 1)
                for b in range(UB):
                    for k in range(K):
                        nc.gpsimd.indirect_dma_start(
                            sorted_rows[n], bass.IndirectOffsetOnAxis(slot[:, us, b, k:k + 1], axis=0),
                            rows[:, us * UB + b, k, :], None).then_inc(scattered[us], 16)

            pool.wait_ge(consts_ready, CONSTS)
            root_x(1)
            pool.wait_ge(bias_ready, 1)
            residual(0, 0, 16)
            residual(1, 1, 16)
            for e in range(E):
                pool.wait_ge(gu_loaded[e], 32)
                nc.gpsimd.tensor_copy(wgu_hi[:, e, :], gu_stage[e]).then_inc(gu_hi_done, 1)
                pool.wait_ge(gu_hi_done, e + 1)
                nc.gpsimd.tensor_tensor(wgu_lo[:, e, :], gu_stage[e], wgu_hi[:, e, :].bitcast(F32),
                                        ALU.subtract).then_inc(gu_split, 1)

            def body(bd):
                for j in range(STEPS):
                    if j % OB == 0 and not (bd.first and j == 0):
                        root_x2(bd.batch(j // OB - 1))
                    if j % 4 == 2 and not (bd.first and j < 4):
                        count_unit(bd.unit(j // 4 - 1), (j // 4 + 1) % BU)
                    if j % 4 == 2 and not bd.last:
                        residual(bd.unit(j // 4 + 2), j // 4, 16 * bd.it + 32)
                    if j % 4 == 0 and not bd.last:
                        root_x(bd.unit(j // 4 + 2))
                    if j % 4 == 3:
                        us = j // 4
                        ru = bd.unit(us - 1)
                        if bd.last and us == BU - 1:
                            root_x2(B - 1)
                        if not (bd.first and us == 0):
                            scatter_unit(ru, (us + 1) % BU, None if bd.first or (bd.second and us == 0) else
                                         16 * UB * K * (bd.it + (us - 1)), 1 if bd.last and us == BU - 1 else 0)

            body(FIRST)
            body(SECOND)
            with pool.Fori(2, NBODY - 1) as it:
                body(Body(it))
            body(LAST)
            pool.wait_ge(pads_written, 16 * E)
            pool.wait_ge(spare_written, 16)
            pad_places(1)

            def scatter_results(it):
                for r in range(RING):
                    wait_apart(pool, y_ready, RING * it + (r + 1))
                    nc.gpsimd.indirect_dma_start(results, bass.IndirectOffsetOnAxis(places[:, r:r + 1], axis=0),
                                                 y[:, r, :], None)\
                      .then_inc(y_scattered[r], 16)

            with pool.Fori(0, LATE_AT + 1) as it:
                scatter_results(it)
            scatter_unit(NUNIT - 1, BU - 1, 16 * UB * K * (NBODY - 1), 1)
            with pool.Fori(LATE_AT + 1, TB) as it:
                scatter_results(it)

        @block.scalar
        def _(act):
            act.dma_start(gates[:, 0:1], g_xattn.partition_broadcast(P)).then_inc(small_loaded, 16)
            act.dma_start(gates[:, 1:2], g_ffn.partition_broadcast(P)).then_inc(small_loaded, 16)
            act.dma_start(bo_b[:, :], bo.partition_broadcast(P)).then_inc(small_loaded, 16)
            act.dma_start(rw_in[:, :], router_w).then_inc(small_loaded, 16)

            def high_weights(w, half):
                if w == 0:
                    f = prologue_fill("WQ", half)
                    act.wait_ge(pj_full, f.full)
                    bank = fill_ps[f.bank]
                else:
                    act.wait_ge(w_full, half + 1)
                    bank = wk_ps[half]
                nc.scalar.copy(w_hi[w][:, half * 512:half * 512 + 512], bank[:, :]).then_inc(w_hi_ready, 1)

            def high_values(part):
                act.wait_ge(w_full, 4 + part + 1)
                nc.scalar.copy(wvo_hi[:, part * 512:part * 512 + 512], vo_ps[part % 2][:, :]).then_inc(w_hi_ready, 1)

            def move(name, part, f, us, when=None):
                if name not in ("XT", "QK", "V", "X2T") or name in ("QK", "V") and on_vector(when, part):
                    return
                act.wait_ge(pj_full, f.full)
                if name == "XT":
                    nc.scalar.copy(xcT_hi[:, :], fill_ps[f.bank][:, :]).then_inc(xcT_hi_ready, 1)
                elif name == "QK" and part % 2 == 0:
                    nc.scalar.activation(projected(name, part, us), fill_ps[f.bank][:, :], ACT.Copy, scale=SCALE)\
                      .then_inc(pj_moved[f.bank], 1)
                elif name in ("QK", "V"):
                    nc.scalar.copy(projected(name, part, us), fill_ps[f.bank][:, :]).then_inc(pj_moved[f.bank], 1)
                elif name == "X2T":
                    nc.scalar.copy(x2T[:, :], fill_ps[f.bank][:, 0:P]).then_inc(pj_moved[f.bank], 1)

            def exp_quad(n, c, par, early=False):
                if not early:
                    act.wait_ge(transposed[c], n - 1)
                    act.wait_ge(probs_ready[c], n)
                act.wait_ge(max_ready[c], n + 1)
                for i in range(4):
                    op = nc.scalar.activation(p_buf[:, c, par, i * P:(i + 1) * P], s_ps[c][:, i * P:(i + 1) * P], ACT.Exp,
                                              bias=neg_max[c][:, i:i + 1], scale=1.0, accum_out=sums[c][:, i:i + 1])
                op.then_inc(exp_ready[c], 1)

            def move_transposed(n, c, par, early=False):
                act.wait_ge(transposed[c], n + 1)
                if not early:
                    act.wait_ge(pv_done[c], n - 1)
                nc.scalar.copy(pT_buf[:, c, par, :], t_ps[c][:, :]).then_inc(probsT_ready[c], 1)

            def gate_exps(u, us):
                act.wait_ge(chosen_ready, u + 1)
                nc.scalar.activation(g_exp[:, us, :, :], topv[:, us, :, 0:K], ACT.Exp, scale=-1.0).then_inc(gate_exp, 1)

            for half in range(2):
                high_weights(0, half)
            move("XT", 0, prologue_fill("XT", 0), 0)
            for half in range(2):
                high_weights(1, half)
            act.wait_ge(small_loaded, 64)
            nc.scalar.activation(tgates[:, :], gates[:, :], ACT.Tanh).then_inc(gates_ready, 1)
            for k in range(4):
                move("QK", k, prologue_fill("QK", k), 0)
            for c in range(2):
                exp_quad(0, c, 0, early=True)
                high_values(2 * c)
                high_values(2 * c + 1)
                for k in range(2):
                    move("QK", 4 + 2 * c + k, prologue_fill("QK", 4 + 2 * c + k), 0)
            move("V", 0, prologue_fill("V", 0), 0)

            def body(bd):
                for j in range(STEPS):
                    n = bd.octet(j)
                    more = not (bd.last and j == STEPS - 1)

                    def run(s):
                        for name, part, _, f in bd.slot(j, s):
                            move(name, part, f, bd.unit_of(name, part, j), s)

                    run("A")
                    if more:
                        exp_quad(n + 1, 0, (j + 1) % 2, early=bd.first and j == 0)
                    for c in range(2):
                        move_transposed(n, c, j % 2, early=bd.first and j < 2)
                    run("B")
                    if more:
                        exp_quad(n + 1, 1, (j + 1) % 2, early=bd.first and j == 0)
                    run("C")
                    if j % 4 == 2 and not (bd.first and j < 4):
                        gate_exps(bd.unit(j // 4 - 1), (j // 4 + 1) % BU)

            body(FIRST)
            with act.Fori(1, NBODY - 1) as it:
                body(Body(it))
            body(LAST)

            def bring_silu():
                nc.scalar.activation(scrap[:, :], tgates[:, 0:1], ACT.Silu).then_inc(table_in, 1)

            bring_silu()

            def high(t, r):
                act.wait_ge(xt_turned, t + 1)
                if not (isinstance(t, int) and t < 2):
                    act.wait_ge(gu_done, t - 1)
                nc.scalar.copy(xtT_hi[:, r % 2, :], xt_ps[:, 0:P]).then_inc(xt_hi_ready, 1)

            def gate(t, r):
                act.wait_ge(gu_done, t + 1)
                if not (isinstance(t, int) and t < 2):
                    act.wait_ge(hid_ready, t - 1)
                nc.scalar.activation(silu[:, r % 2, :], gu_ps[r % 2][:, 0:F], ACT.Silu).then_inc(silu_ready, 1)

            def move_hidden(t, r):
                act.wait_ge(hid_turned, t + 1)
                if not (isinstance(t, int) and t < 2):
                    act.wait_ge(down_done, t - 1)
                nc.scalar.copy(hidT[:, r % 2, :], ht_ps[r % 2][:, 0:F]).then_inc(hidT_ready, 1)

            def tiles_body(it, first=False, last=False, between=None):
                for r in range(RING):
                    t = RING * it + r
                    if r == RING // 2 and between:
                        between()
                    if not (last and r == RING - 1):
                        high(t + 1, r + 1)
                    gate(t, r)
                    if not (first and r == 0):
                        move_hidden(t - 1, r - 1)

            high(0, 0)
            tiles_body(0, first=True)
            tiles_body(1, between=lambda: move("X2T", 0, LateFill(0), None))
            tiles_body(2)
            gate_exps(NUNIT - 1, BU - 1)
            act.wait_ge(table_in, 1)
            bring_silu()
            with act.Fori(3, TB - 1) as it:
                tiles_body(it)
            tiles_body(TB - 1, last=True)
            move_hidden(T - 1, T - 1)

            for g in range(NG):
                act.wait_ge(total_ready, g + 1)
                act.dma_start(out[g * GT:(g + 1) * GT].rearrange("b t d -> t b d"),
                              y12[:, g, 1, :].rearrange("p (b d) -> p b d", b=GT)).then_inc(out_stored, 16)
            act.wait_ge(out_stored, 16 * NG)

        @block.tensor
        def _(pe):
            def claim(f):
                if f.before is not None:
                    pe.wait_ge(pj_moved[f.bank], f.before)
                return fill_ps[f.bank]

            pe.wait_ge(ident_ready, 1)

            def turn_weights(w, bank_of, done):
                pe.wait_ge(w_loaded[w], 16)
                for half in range(2):
                    bank = bank_of(half)
                    for c in range(4):
                        mm = nc.tensor.transpose(bank[:, c * P:(c + 1) * P], w_stage[w][:, 4 * half + c, :], ident[:, :])
                    mm.then_inc(done, 1)

            def value_weights(part):
                pe.wait_ge(w_moved, 4 if part < 2 else 4 + part - 1)
                for i in range(4):
                    c, row = part // 2 * 4 + i, slice(part % 2 * HD, (part % 2 + 1) * HD)
                    mm = nc.tensor.matmul(vo_ps[part % 2][:, i * P:(i + 1) * P], w_stage[2][row, c, :], woT[row, c, :],
                                          start=True, stop=True)
                mm.then_inc(w_full, 1)

            def product(outp, lhs, rhs):
                (lh, ll), (rh, rl) = lhs, rhs
                nc.tensor.matmul(outp, ll, rh, start=True, stop=False)
                nc.tensor.matmul(outp, lh, rl, start=False, stop=False)
                return nc.tensor.matmul(outp, lh, rh, start=False, stop=True)

            def so_far():
                return counted[:, UB, :].unsqueeze(1).to_broadcast([P, UB, E])

            def fill(name, part, b, f, us, bd):
                bank = claim(f)
                if name == "XT":
                    u = us if bd is None else bd.unit(us)
                    pe.wait_ge(xn_ready, u + 1)
                    pe.wait_ge(c_loaded[us % 2], 16 * (0 if bd is None else bd.it) + 16 * (us // 2 + 1))
                    for i in range(UB):
                        mm = nc.tensor.transpose(bank[:, (UB + i) * P:(UB + i + 1) * P], c_in[us % 2][:, i, :], ident[:, :])
                    mm.then_inc(ctxT_taken, 1)
                    for i in range(UB):
                        mm = nc.tensor.transpose(bank[:, i * P:(i + 1) * P], xn[us % 2][:, i, :], ident[:, :])
                elif name == "QK":
                    if part == 0:
                        wait_moved(pe, [prologue_fill("XT", 0) if bd is None else bd.ahead("XT", 0, us)])
                    src = slice(0, UB * P) if part % 2 == 0 else slice(UB * P, 2 * UB * P)
                    for i in range(2):
                        c = part // 2 * 2 + i
                        w = part % 2
                        mm = product(bank[:, i * 256:i * 256 + 256],
                                     [t[:, c * P:(c + 1) * P] for t in (w_hi[w], w_lo[w])],
                                     [t[:, src] for t in (xcT_hi, xcT_lo)])
                elif name == "V":
                    tok = slice((UB + part // 4) * P, (UB + part // 4 + 1) * P)
                    feat = slice(part % 4 * 512, part % 4 * 512 + 512)
                    mm = product(bank[:, :], [t[:, tok] for t in (xcT_hi, xcT_lo)], [t[:, feat] for t in (wvo_hi, wvo_lo)])
                elif name == "X2T":
                    pe.wait_ge(x2_ready, b + 1)
                    mm = nc.tensor.transpose(bank[:, 0:P], rows[:, us % BB, 0, 0:P], ident[:, :])
                elif name == "LG":
                    mm = nc.tensor.matmul(bank[:, 0:E], x2T[:, :], rwT[:, :], start=True, stop=True)
                elif name == "RK":
                    pe.wait_ge(counted_ready, b + 1)
                    nc.tensor.matmul(bank[:, 0:UB * E], before[:, :], count[:, :, :].rearrange("p b e -> p (b e)"),
                                     start=True, stop=False)
                    mm = nc.tensor.matmul(bank[:, 0:UB * E], ones[:, :],
                                          counted[:, 0:UB, :].rearrange("p b e -> p (b e)"), start=False, stop=True)
                elif name == "LAST RK":
                    pe.wait_ge(last_count, 1)
                    nc.tensor.matmul(bank[:, 0:UB * E], before[:, :], count[:, :, :].rearrange("p b e -> p (b e)"),
                                     start=True, stop=False)
                    nc.tensor.matmul(bank[:, E:UB * E], ones[:, :], count[:, 0, :], start=False, stop=False)
                    nc.tensor.matmul(bank[:, 0:UB * E], ones[:, :], so_far(), start=False, stop=True)
                    for i in range(UB):
                        nc.tensor.matmul(bank[:, UB * E:(UB + 1) * E], ones[:, :], count[:, i, :], start=i == 0, stop=False)
                    mm = nc.tensor.matmul(bank[:, UB * E:(UB + 1) * E], ones[:, :], counted[:, UB, :], start=False, stop=True)
                elif name == "CT":
                    mm = nc.tensor.matmul(bank[:, 0:E], ones[:, :], counted[:, UB, :], start=True, stop=True)
                mm.then_inc(pj_full, 1)

            def scores(n, bs, o, us, needs, first=False):
                wait_moved(pe, needs)
                for c in range(2):
                    if not first:
                        pe.wait_ge(exp_ready[c], n)
                q, k = (qkT[:, us % 2, w, :, :] for w in range(2))
                tok = slice(bs * P, (bs + 1) * P)
                for i in range(4):
                    for c in range(2):
                        rows = slice(c * HD, (c + 1) * HD)
                        mm = nc.tensor.matmul(s_ps[c][:, i * P:(i + 1) * P], q[rows, 4 * o + i, tok],
                                              k[rows, 4 * o + i, tok], start=True, stop=True)
                        if i == 3:
                            mm.then_inc(scored[c], 1)

            def transposes(n, par, first=False):
                for c in range(2):
                    pe.wait_ge(probs_ready[c], n + 1)
                    if not first:
                        pe.wait_ge(probsT_ready[c], n)
                    for i in range(4):
                        mm = nc.tensor.transpose(t_ps[c][:, i * P:(i + 1) * P], p_buf[:, c, par, i * P:(i + 1) * P],
                                                 ident[:, :])
                    mm.then_inc(transposed[c], 1)

            def values(n, b, slot, o, par, needs, early=False):
                wait_moved(pe, needs)
                if o == 0 and not early:
                    pe.wait_ge(x1_ready, b - 1)
                for c in range(2):
                    pe.wait_ge(probsT_ready[c], n + 1)
                    for i in range(4):
                        mm = nc.tensor.matmul(o_ps[slot][:, 0:P], pT_buf[:, c, par, i * P:(i + 1) * P],
                                              v[:, slot, 8 * o + 4 * c + i, :], start=o == 0 and c == 0 and i == 0,
                                              stop=o == OB - 1 and c == 1 and i == 3)
                    mm.then_inc(pv_done[c], 1)

            turn_weights(0, lambda half: claim(prologue_fill("WQ", half)), pj_full)
            fill("XT", 0, None, prologue_fill("XT", 0), 0, None)
            turn_weights(1, lambda half: wk_ps[half], w_full)
            turn_weights(3, lambda half: wo_ps[half], w_full)
            wait_moved(pe, [prologue_fill("WQ", half) for half in range(2)])
            pe.wait_ge(w_moved, 2)
            for k in range(4):
                fill("QK", k, None, prologue_fill("QK", k), 0, None)
            scores(0, 0, 0, 0, [prologue_fill("QK", k) for k in range(4)], first=True)
            pe.wait_ge(w_loaded[2], 16)
            for h in range(2):
                for part in range(2):
                    value_weights(2 * h + part)
                for k in range(2):
                    fill("QK", 4 + 2 * h + k, None, prologue_fill("QK", 4 + 2 * h + k), 0, None)
            f = prologue_fill("RW", 0)
            bank = claim(f)
            pe.wait_ge(small_loaded, 64)
            nc.tensor.transpose(bank[:, 0:E], rw_in[:, :], ident[0:E, 0:E]).then_inc(pj_full, 1)
            wait_moved(pe, [prologue_fill("RW", 0)])
            pe.wait_ge(w_moved, 8)
            fill("V", 0, None, prologue_fill("V", 0), 0, None)
            pe.wait_ge(consts_ready, CONSTS)

            def body(bd):
                for j in range(STEPS):
                    n = bd.octet(j)
                    if not (bd.last and j == STEPS - 1):
                        m = j + 1
                        o = m % OB
                        scores(n + 1, m // OB % UB, o, m // 4, [bd.ahead("QK", k, m // 4) for k in range(4 * o, 4 * o + 4)])

                    def run(s):
                        for name, part, bb, f in bd.slot(j, s):
                            if name == "LG":
                                wait_moved(pe, [bd.find("X2T", 0, [j])])
                            if name == "RK":
                                fill(name, part, bd.unit(bb), f, bb, bd)
                            elif bb is not None:
                                fill(name, part, bd.batch(bb), f, bb, bd)
                            else:
                                fill(name, part, None, f, bd.unit_of(name, part, j), bd)

                    run("A")
                    transposes(n, j % 2, first=bd.first and j == 0)
                    run("B")
                    bb, o = divmod(j, OB)
                    values(n, bd.batch(bb), bb % UB, o, j % 2,
                           [bd.ahead("V", 4 * (bb % UB) + 2 * o + h, j // 4) for h in range(2)], early=bd.first and bb < UB)
                    run("C")

            body(FIRST)
            with pe.Fori(1, NBODY - 1) as it:
                body(Body(it))
            body(LAST)

            pe.wait_ge(gu_split, E)
            pe.wait_ge(wd_loaded, 16)
            pe.wait_ge(plan, PLAN_STEPS)
            for c in range(2):
                pe.wait_ge(exp_ready[c], NOCT)
                pe.wait_ge(probsT_ready[c], NOCT)
            pe.wait_ge(x1_ready, B)
            wait_moved(pe, [Fill(TAIL - 2), Fill(TAIL - 1)])

            def turn(t, r, arrived):
                pe.wait_ge(xt_loaded[r % RING], arrived)
                if not (isinstance(t, int) and t < 1):
                    pe.wait_ge(xt_ready, t)
                nc.tensor.transpose(xt_ps[:, 0:P], xt[:, r % RING, 0:P], ident[:, :]).then_inc(xt_turned, 1)

            wgu_flat = [w[:, :, :].rearrange("p e f -> p (e f)") for w in (wgu_hi, wgu_lo)]
            wd_flat = wd[:, :, :, :].rearrange("p e c d -> p (e c d)")

            def gate_up(t, r, e):
                pe.wait_ge(xt_ready, t + 1)
                if not (isinstance(t, int) and t < 2):
                    pe.wait_ge(hid_ready, t - 1)
                product(gu_ps[r % 2][:, :], [x[:, r % 2, :] for x in (xtT_hi, xtT_lo)],
                        [w[:, bass.ds(e * (2 * F), 2 * F)] for w in wgu_flat]).then_inc(gu_done, 1)

            def turn_hidden(t, r):
                pe.wait_ge(hid_ready, t + 1)
                if not (isinstance(t, int) and t < 2):
                    pe.wait_ge(hidT_ready, t - 1)
                for c in range(FC):
                    mm = nc.tensor.transpose(ht_ps[r % 2][:, c * P:(c + 1) * P], hid[:, r % 2, c * P:(c + 1) * P], ident[:, :])
                mm.then_inc(hid_turned, 1)

            def down(t, r, e):
                pe.wait_ge(hidT_ready, t + 1)
                if not (isinstance(t, int) and t < 2):
                    pe.wait_ge(y_ready, t - 1)
                for c in range(FC):
                    mm = nc.tensor.matmul(y_ps[r % 2][:, 0:P], hidT[:, r % 2, c * P:(c + 1) * P],
                                          wd_flat[:, bass.ds(e * (FC * P) + c * P, P)], start=c == 0, stop=c == FC - 1)
                mm.then_inc(down_done, 1)

            def tiles_body(it, first=False, last=False, between=None):
                experts = load_values(expert_of[0:1, bass.ds(it * RING, BEHIND + RING)], mybir.EngineType.PE, E - 1)
                for r in range(RING):
                    t = RING * it + r
                    if r == RING // 2 and between:
                        between()
                    if not (last and r == RING - 1):
                        turn(t + 1, r + 1, 16 * (it + (r + 1) // RING) + 16)
                    gate_up(t, r, experts[BEHIND + r])
                    if not (first and r < 1):
                        turn_hidden(t - 1, r - 1)
                    if not (first and r < 2):
                        down(t - 2, r - 2, experts[BEHIND + r - 2])
                return experts

            turn(0, 0, 16)
            tiles_body(0, first=True)
            tiles_body(1, between=lambda: fill("X2T", 0, B - 1, LateFill(0), BB - 1, None))
            wait_moved(pe, [LateFill(0)])
            fill("LG", 0, B - 1, LateFill(1), None, None)
            tiles_body(2)
            fill("LAST RK", 0, NUNIT - 1, LateFill(2), None, None)
            with pe.Fori(3, NTB[0]) as it:
                tiles_body(it)
            pe.wait_ge(plan, 2 * PLAN_STEPS)
            with pe.Fori(NTB[0], TB - 1) as it:
                tiles_body(it)
            experts = tiles_body(TB - 1, last=True)
            turn_hidden(T - 1, T - 1)
            down(T - 2, T - 2, experts[BEHIND + RING - 2])
            down(T - 1, T - 1, experts[BEHIND + RING - 1])

        @block.vector
        def _(dve):
            def stats_x(u, par, arrived):
                dve.wait_ge(x_loaded[par], arrived)
                for i in range(UB):
                    op = nc.vector.bn_stats(st1[:, i, :], x_in[par][:, i, :])
                op.then_inc(stats1, 1)
                wait_apart(dve, stats1, u + 1)
                for i in range(UB):
                    nc.vector.bn_aggr(mv1[:, i, :], st1[:, i, :]).then_inc(agg1, 1)

            def norm_x(u, par):
                dve.wait_ge(rstd1, u + 1)
                for i in range(UB):
                    op = nc.vector.tensor_scalar(xn[par][:, i, :], x_in[par][:, i, :], mv1[:, i, 0:1],
                                                 rs1[:, i:i + 1], ALU.subtract, ALU.mult)
                op.then_inc(xn_ready, 1)

            def norm_x2(b, s, earlier):
                dve.wait_ge(rstd2, b + 1)
                if earlier is not None:
                    dve.wait_ge(scattered[s // UB], earlier)
                for k in range(K):
                    op = nc.vector.tensor_scalar(rows[:, s, k, 0:P], x1_all[:, bass.ds(b * P, P)], mv2[:, 0:1],
                                                 rs2[:, :], ALU.subtract, ALU.mult)
                op.then_inc(x2_ready, 1)

            def select(u, us, logits):
                for f in logits:
                    wait_apart(dve, pj_moved[f.bank], f.moved)
                for b in range(UB):
                    op = nc.vector.max(topv[:, us, b, :], lg[:, us * UB + b, :])
                op.then_inc(top_ready, 1)
                wait_apart(dve, top_ready, u + 1)
                for b in range(UB):
                    op = nc.vector.max_index(topi[:, us, b, :], topv[:, us, b, :], lg[:, us * UB + b, :])
                op.then_inc(topi_ready, 1)
                dve.wait_ge(topi_ready, u + 1)
                nc.vector.tensor_copy(topf[:, :, :], topi[:, us, :, 0:K]).then_inc(topf_ready, 1)
                dve.wait_ge(topf_ready, u + 1)
                nc.vector.tensor_tensor(chosen[:, us, :, :, :],
                                        iota_e[:, :].unsqueeze(1).unsqueeze(1).to_broadcast([P, UB, K, E]),
                                        topf[:, :, :].unsqueeze(3).to_broadcast([P, UB, K, E]), ALU.is_equal)\
                  .then_inc(chosen_ready, 1)

            def gate_unit(u, us):
                dve.wait_ge(gate_exp, u + 1)
                nc.vector.tensor_scalar(g_exp[:, us, :, :], g_exp[:, us, :, :], 1.0, None, ALU.add).then_inc(gate_chain, 1)
                dve.wait_ge(gate_chain, 4 * u + 1)
                nc.vector.reciprocal(g_sig[:, :, :], g_exp[:, us, :, :]).then_inc(gate_chain, 1)
                dve.wait_ge(gate_chain, 4 * u + 2)
                nc.vector.scalar_tensor_tensor(out=g_sum[:, :], in0=g_sig[:, :, 0], scalar=1e-10, in1=g_sig[:, :, 1],
                                               op0=ALU.add, op1=ALU.add).then_inc(gate_chain, 1)
                dve.wait_ge(gate_chain, 4 * u + 3)
                nc.vector.reciprocal(g_sum[:, :], g_sum[:, :]).then_inc(gate_chain, 1)
                dve.wait_ge(gate_chain, 4 * u + 4)
                nc.vector.scalar_tensor_tensor(out=rows[:, us * UB:(us + 1) * UB, :, GATE], in0=g_sig[:, :, :],
                                               scalar=tgates[:, 1:2],
                                               in1=g_sum[:, :].unsqueeze(2).to_broadcast([P, UB, K]),
                                               op0=ALU.mult, op1=ALU.mult).then_inc(gates_done, 1)

            def low_weights(w, half):
                at = slice(half * 512, half * 512 + 512)
                f = prologue_fill("WQ", half)
                bank, done = (fill_ps[f.bank], pj_moved[f.bank]) if w == 0 else (wk_ps[half], w_moved)
                dve.wait_ge(w_hi_ready, 2 * w + half + 1)
                nc.vector.tensor_tensor(w_lo[w][:, at], bank[:, :], w_hi[w][:, at].bitcast(F32), ALU.subtract)\
                  .then_inc(done, 1)

            def low_values(part):
                at = slice(part * 512, part * 512 + 512)
                dve.wait_ge(w_hi_ready, 4 + part + 1)
                nc.vector.tensor_tensor(wvo_lo[:, at], vo_ps[part % 2][:, :], wvo_hi[:, at].bitcast(F32), ALU.subtract)\
                  .then_inc(w_moved, 1)

            def move(name, part, f, u, when=None, us=0):
                if name in ("QK", "V"):
                    if on_vector(when, part):
                        dve.wait_ge(pj_full, f.full)
                        if name == "QK" and part % 2 == 0:
                            nc.vector.tensor_scalar(projected(name, part, us), fill_ps[f.bank][:, :], SCALE, None, ALU.mult)\
                              .then_inc(pj_moved[f.bank], 1)
                        else:
                            nc.vector.tensor_copy(projected(name, part, us), fill_ps[f.bank][:, :]).then_inc(pj_moved[f.bank], 1)
                elif name == "XT":
                    dve.wait_ge(xcT_hi_ready, u + 1)
                    nc.vector.tensor_tensor(xcT_lo[:, :], fill_ps[f.bank][:, :], xcT_hi[:, :].bitcast(F32), ALU.subtract)\
                      .then_inc(pj_moved[f.bank], 1)
                elif name == "LG":
                    dve.wait_ge(pj_full, f.full)
                    nc.vector.tensor_copy(lg[:, u, :], fill_ps[f.bank][:, 0:E]).then_inc(pj_moved[f.bank], 1)
                elif name == "CT":
                    dve.wait_ge(pj_full, f.full)
                    nc.vector.tensor_copy(row_ends[:, :], fill_ps[f.bank][:, 0:E]).then_inc(pj_moved[f.bank], 1)
                elif name == "RK":
                    dve.wait_ge(pj_full, f.full)
                    rank = fill_ps[f.bank][:, 0:UB * E].rearrange("p (b e) -> p b e", e=E)
                    nc.vector.tensor_tensor(ranked[:, :, :, :], rank.unsqueeze(2).to_broadcast([P, UB, K, E]),
                                            chosen[:, u, :, :, :], ALU.mult).then_inc(pj_moved[f.bank], 1)
                    dve.wait_ge(pj_moved[f.bank], f.moved)
                    with nc.allow_low_precision(reason="whole numbers below 2^24 are exact in float32"):
                        nc.vector.tensor_reduce(slot[:, u, :, :], ranked[:, :, :, :], AX.X, ALU.add).then_inc(slots_ready, 1)

            def add_attention(b, par):
                x1 = x1_all[:, bass.ds(b * P, P)]
                dve.wait_ge(pv_done[1], OB * (b + 1))
                dve.wait_ge(xb_ready, NUNIT if isinstance(b, int) and b == B - 1 else b // UB + 1)
                nc.vector.scalar_tensor_tensor(out=x1, in0=o_ps[par][:, 0:P], scalar=tgates[:, 0:1], in1=x1,
                                               op0=ALU.mult, op1=ALU.add).then_inc(x1_ready, 1)
                wait_apart(dve, x1_ready, b + 1)
                nc.vector.bn_stats(st2[:, :], x1).then_inc(stats2, 1)
                wait_apart(dve, stats2, b + 1)
                nc.vector.bn_aggr(mv2[:, :], st2[:, :]).then_inc(agg2, 1)

            steps = [0]

            def step(op):
                op.then_inc(plan, 1)
                steps[0] += 1
                dve.wait_ge(plan, steps[0])

            def count_tiles(n):
                step(nc.vector.tensor_copy(pads_at[:, n, :], row_ends[:, :]))
                step(nc.vector.tensor_tensor(ends[:, :], row_ends[:, :], region_at[:, n, :], ALU.subtract))
                step(nc.vector.tensor_tensor(tiles_tmp[:, :, 0:NOF[n]], ends[:, :].unsqueeze(2).to_broadcast([P, E, NOF[n]]),
                                             thresholds[:, :, 0:NOF[n]], ALU.is_gt))
                step(nc.vector.tensor_reduce(tiles[:, :], tiles_tmp[:, :, 0:NOF[n]], AX.X, ALU.add))
                step(nc.vector.tensor_tensor(tiles_tmp2[:, :, :], tiles[:, :].unsqueeze(1).to_broadcast([P, E, E]),
                                             upto[:, :, :], ALU.mult))
                step(nc.vector.tensor_reduce(tiles_upto[:, :], tiles_tmp2[:, :, :], AX.X, ALU.add))

            def find_experts(n):
                at = BEHIND + sum(NT[:n])
                p = past[:, 0:NT[n], :]
                step(nc.vector.tensor_tensor(p, tiles_upto[:, :].unsqueeze(1).to_broadcast([P, NT[n], E]),
                                             iota_t[:, 0:NT[n], :], ALU.is_le))
                step(nc.vector.tensor_reduce(tile_e[:, 0:NT[n]], p, AX.X, ALU.add))
                step(nc.vector.tensor_scalar(expert_of[:, at:at + NT[n]], tile_e[:, 0:NT[n]], float(E - 1), None, ALU.min))

            def find_first_rows(n):
                at = sum(NT[:n])
                p, e = past[:, 0:NT[n], :], tile_e[:, 0:NT[n]]
                step(nc.vector.tensor_tensor(p, p, tiles[:, :].unsqueeze(1).to_broadcast([P, NT[n], E]), ALU.mult))
                step(nc.vector.tensor_reduce(tile_before[:, 0:NT[n]], p, AX.X, ALU.add))
                step(nc.vector.scalar_tensor_tensor(out=e, in0=e, scalar=float(REGION[n]), in1=row_t[:, 0:NT[n]],
                                                    op0=ALU.mult, op1=ALU.add))
                step(nc.vector.scalar_tensor_tensor(out=first_row[:, at:at + NT[n]], in0=tile_before[:, 0:NT[n]],
                                                    scalar=-float(P), in1=e, op0=ALU.mult, op1=ALU.add))
                assert steps[0] == PLAN_STEPS * (n + 1)

            def find_max(n, c):
                s = s_ps[c][:, :].rearrange("p (h k) -> p h k", h=4)
                dve.wait_ge(scored[c], n + 1)
                nc.vector.tensor_reduce(neg_max[c][:, :], s, AX.X, ALU.max, negate=True).then_inc(max_ready[c], 1)

            def normalize(n, c, par):
                p = p_buf[:, c, par, :].rearrange("p (h k) -> p h k", h=4)
                dve.wait_ge(exp_ready[c], n + 1)
                nc.vector.reciprocal(rden[c][:, :], sums[c][:, :]).then_inc(rden_ready[c], 1)
                dve.wait_ge(rden_ready[c], n + 1)
                nc.vector.tensor_tensor(p, p, rden[c][:, :].unsqueeze(2).to_broadcast([P, 4, P]), ALU.mult)\
                  .then_inc(probs_ready[c], 1)

            stats_x(0, 0, 16)
            norm_x(0, 0)
            for half in range(2):
                low_weights(0, half)
            move("XT", 0, prologue_fill("XT", 0), 0)
            for half in range(2):
                low_weights(1, half)
            for half in range(2):
                dve.wait_ge(w_full, 2 + half + 1)
                nc.vector.tensor_copy(woT[:, 4 * half:4 * half + 4, :].rearrange("p c d -> p (c d)"), wo_ps[half][:, :])\
                  .then_inc(w_moved, 1)
            for k in range(4):
                move("QK", k, prologue_fill("QK", k), 0)
            stats_x(1, 1, 16)
            for c in range(2):
                find_max(0, c)
            dve.wait_ge(small_loaded, 64)
            dve.wait_ge(gates_ready, 1)
            nc.vector.tensor_scalar(bo_t[:, :], bo_b[:, :], tgates[:, 0:1], None, ALU.mult).then_inc(bias_ready, 1)
            for c in range(2):
                low_values(2 * c)
                low_values(2 * c + 1)
                for k in range(2):
                    move("QK", 4 + 2 * c + k, prologue_fill("QK", 4 + 2 * c + k), 0)
                normalize(0, c, 0)
            f = prologue_fill("RW", 0)
            dve.wait_ge(pj_full, f.full)
            nc.vector.tensor_copy(rwT[:, :], fill_ps[f.bank][:, 0:E]).then_inc(pj_moved[f.bank], 1)
            norm_x(1, 1)

            def body(bd):
                for j in range(STEPS):
                    n = bd.octet(j)
                    more = not (bd.last and j == STEPS - 1)
                    bb = j // OB - 1
                    if more:
                        for c in range(2):
                            find_max(n + 1, c)
                    else:
                        find_first_rows(0)

                    def run(s):
                        for name, part, at, f in bd.slot(j, s):
                            if name == "RK":
                                move(name, part, f, at % BU)
                            elif name == "LG":
                                move(name, part, f, at % BB)
                            else:
                                move(name, part, f, bd.unit(j // 4 + 1), s, bd.unit_of(name, part, j))

                    run("A")
                    if bd.last and j == UB * OB + 1:
                        f = bd.find("CT", 0, [UB * OB])
                        dve.wait_ge(pj_moved[f.bank], f.moved)
                        count_tiles(0)
                    if j % 4 == 2 and not (bd.first and j < 4):
                        select(bd.unit(j // 4 - 1), (j // 4 + 1) % BU, [bd.find("LG", 0, [j - k]) for k in (3, 1)])
                    run("B")
                    if more:
                        for c in range(2):
                            normalize(n + 1, c, (j + 1) % 2)
                            if bd.last and j == UB * OB + 2 and c == 0:
                                find_experts(0)
                    if j % OB == 1:
                        add_attention(bd.batch(j // OB), j // OB % 2)
                    run("C")
                    if j % 4 == 3 and not (bd.first and j < 4):
                        gate_unit(bd.unit(j // 4 - 1), (j // 4 + 1) % BU)
                    if j % OB == 0 and not (bd.first and bb < 0):
                        norm_x2(bd.batch(bb), bb % BB, None if bd.first or (bd.second and bb < 0) else
                                16 * UB * K * (bd.it + (-1 if bb < 0 else 0)))
                    if j % 4 == 1 and not bd.last:
                        norm_x(bd.unit(j // 4 + 2), j // 4)
                    if j % 4 == 0 and not bd.last:
                        us = j // 4
                        stats_x(bd.unit(us + 2), us, 16 * bd.it + 32)

            body(FIRST)
            body(SECOND)
            with dve.Fori(2, NBODY - 1) as it:
                body(Body(it))
            body(LAST)

            def low(t, r):
                dve.wait_ge(xt_hi_ready, t + 1)
                nc.vector.tensor_tensor(xtT_lo[:, r % 2, :], xt_ps[:, 0:P], xtT_hi[:, r % 2, :].bitcast(F32),
                                        ALU.subtract).then_inc(xt_ready, 1)

            def hidden(t, r):
                dve.wait_ge(silu_ready, t + 1)
                if not (isinstance(t, int) and t < 2):
                    dve.wait_ge(hid_turned, t - 1)
                nc.vector.tensor_tensor(hid[:, r % 2, :], silu[:, r % 2, :], gu_ps[r % 2][:, F:2 * F], ALU.mult)\
                  .then_inc(hid_ready, 1)

            def gated(t, r, earlier):
                dve.wait_ge(down_done, t + 1)
                if earlier is not None:
                    dve.wait_ge(y_scattered[r % RING], earlier)
                nc.vector.tensor_copy(places[:, r % RING:r % RING + 1], xt[:, r % RING, DEST:DEST + 1].bitcast(U32))
                nc.vector.tensor_scalar(y[:, r % RING, :], y_ps[r % 2][:, 0:P], xt[:, r % RING, GATE:GATE + 1], None,
                                        ALU.mult).then_inc(y_ready, 1)

            def sum_group(g):
                both = y12[:, g, :, :]
                dve.wait_ge(y12_loaded[g], 16 * K)
                nc.vector.tensor_tensor(both[:, 0, :], x1_all[:, g * GT * P:(g + 1) * GT * P], both[:, 0, :], ALU.add)\
                  .then_inc(part_ready, 1)
                dve.wait_ge(part_ready, g + 1)
                nc.vector.tensor_tensor(both[:, 1, :], both[:, 0, :], both[:, 1, :], ALU.add).then_inc(total_ready, 1)

            def tiles_body(it, first=False, last=False, second=False, between=None):
                for r in range(RING):
                    t = RING * it + r
                    if last and r >= RING - SOON:
                        sum_group(r - (RING - SOON))
                    if r == RING // 2 and between:
                        between()
                    if not (last and r == RING - 1):
                        low(t + 1, r + 1)
                    hidden(t, r)
                    if not (first and r < 2):
                        early = first or (second and r < 2)
                        gated(t - 2, r - 2, None if early else 16 * (it + (-1 if r < 2 else 0)))

            low(0, 0)
            tiles_body(0, first=True)
            norm_x2(B - 1, BB - 1, 16 * UB * K * (NBODY - 1))
            tiles_body(1, second=True)

            def select_last():
                move("LG", 0, LateFill(1), BB - 1)
                select(NUNIT - 1, BU - 1, [LAST.find("LG", 0, [STEPS - 1]), LateFill(1)])
                dve.wait_ge(slots_ready, NUNIT - 1)
                dve.wait_ge(chosen_ready, NUNIT)
                nc.vector.tensor_tensor(count[:, :, :], chosen[:, BU - 1, :, 0, :], chosen[:, BU - 1, :, 1, :], ALU.add)\
                  .then_inc(last_count, 1)

            def rank_last():
                f = LateFill(2)
                dve.wait_ge(pj_full, f.full)
                dve.wait_ge(plan, PLAN_STEPS)
                nc.vector.tensor_copy(row_ends[:, :], fill_ps[f.bank][:, UB * E:(UB + 1) * E]).then_inc(late_ends, 1)
                move("RK", 0, f, BU - 1)

            tiles_body(2, between=select_last)
            tiles_body(3, between=rank_last)
            dve.wait_ge(late_ends, 1)
            count_tiles(1)
            tiles_body(4, between=lambda: gate_unit(NUNIT - 1, BU - 1))
            find_experts(1)
            find_first_rows(1)
            with dve.Fori(5, TB - 1) as it:
                tiles_body(it)
            tiles_body(TB - 1, last=True)
            gated(T - 2, T - 2, 16 * (TB - 1))
            gated(T - 1, T - 1, 16 * (TB - 1))

            for g in range(SOON, NG):
                sum_group(g)


_INS = ["x", "ctx_1024", "g_xattn", "g_ffn", "L0_xattn_Wq", "L0_xattn_Wk", "L0_xattn_Wv", "L0_xattn_Wo", "L0_xattn_bo",
        "L0_ffn_router_w", "L0_ffn_w_gate", "L0_ffn_w_up", "L0_ffn_w_down"]


def kernel(**inputs):
    import numpy as _np
    import concourse.bacc as _bacc
    from concourse import mybir as _mybir
    from concourse.bass_utils import run_bass_kernel_spmd as _run

    nc = _bacc.Bacc("TRN2", target_bir_lowering=False, num_devices=1)
    arrays, args = {}, []
    for name in _INS:
        a = _np.ascontiguousarray(inputs[name])
        arrays[f"in_{name}"] = a
        args.append(nc.dram_tensor(f"in_{name}", a.shape, _mybir.dt.from_np(a.dtype), kind="ExternalInput").ap())
    args.append(nc.dram_tensor("out_0", (B, P, P), F32, kind="ExternalOutput").ap())
    args.append([nc.dram_tensor(f"sorted_rows{n}", (E * REGION[n] + SPARE * P, ROW), F32, kind="Internal").ap()
                 for n in range(len(UNITS))])
    args.append(nc.dram_tensor("results", (NOWHERE + len(UNITS) * (E + SPARE) * P, P), F32, kind="Internal").ap())
    build(nc, *args)
    r = _run(nc, [arrays], core_ids=[0])
    return r.results[0]["out_0"]
```
